# Optimizing a Trainium2 kernel written in Bass

```python
import numpy as np
import jax
import jax.numpy as jnp

def _softmax(x, axis=-1):
    return jax.nn.softmax(x, axis=axis)

def _gelu(x):
    return jax.nn.gelu(x, approximate=True)

def _silu(x):
    return jax.nn.silu(x)

def _sigmoid(x):
    return jax.nn.sigmoid(x)

def _layernorm(x, axis=-1, eps=1e-05):
    m = jnp.mean(x, axis=axis, keepdims=True)
    v = jnp.var(x, axis=axis, keepdims=True)
    return (x - m) / jnp.sqrt(v + eps)

def _scatter_add(tgt, idx, src, axis=0):
    return tgt.at[idx].add(src)

def _segment_sum(src, seg, n):
    return jax.ops.segment_sum(src, seg, n)
kernel_name = 'mk_sandwich_d1_jaxref_r4_8dcafb'

def setup_inputs(seed: int=0):
    np.random.seed(seed)
    _w = jnp.asarray

    def _L0_attn_setup():
        import jax, jax.numpy as jnp
        import numpy as np
        D_MODEL = 256
        D_STATE = 16
        D_CONV = 4
        EXPAND = 2
        BATCH = 2
        SEQLEN = 512
        EPS = 1.1920928955078125e-07

        def _mamba_block(x, norm_w, in_proj_w, conv_w, conv_b, x_proj_w, dt_proj_w, dt_proj_b, A_log, D, out_proj_w):
            B, L, _ = x.shape
            d_inner, K = conv_w.shape
            dt_rank = dt_proj_w.shape[1]
            N = A_log.shape[1]
            h = x * jax.lax.rsqrt(jnp.mean(x * x, axis=-1, keepdims=True) + EPS) * norm_w
            xz = h @ in_proj_w.T
            u, z = jnp.split(xz, 2, axis=-1)
            up = jnp.pad(u, ((0, 0), (K - 1, 0), (0, 0)))
            uc = conv_b + sum((up[:, k:k + L, :] * conv_w[:, k] for k in range(K)))
            uc = jax.nn.silu(uc)
            x_dbl = uc @ x_proj_w.T
            dt, Bm, Cm = jnp.split(x_dbl, [dt_rank, dt_rank + N], axis=-1)
            dt = jax.nn.softplus(dt @ dt_proj_w.T + dt_proj_b)
            A = -jnp.exp(A_log)
            dA = jnp.exp(jnp.einsum('bld,dn->bldn', dt, A))
            dBu = jnp.einsum('bld,bln,bld->bldn', dt, Bm, uc)

            def step(hprev, inputs):
                dA_t, dBu_t, C_t = inputs
                hcur = dA_t * hprev + dBu_t
                y_t = jnp.einsum('bdn,bn->bd', hcur, C_t)
                return (hcur, y_t)
            h0 = jnp.zeros((B, d_inner, N), x.dtype)
            _, ys = jax.lax.scan(step, h0, (dA.transpose(1, 0, 2, 3), dBu.transpose(1, 0, 2, 3), Cm.transpose(1, 0, 2)))
            y = ys.transpose(1, 0, 2) + uc * D
            y = y * jax.nn.silu(z)
            out = y @ out_proj_w.T
            return out + x
        key = jax.random.key(seed)
        d_model, B, L = (D_MODEL, BATCH, SEQLEN)
        d_inner = EXPAND * d_model
        dt_rank = (d_model + 15) // 16
        ks = jax.random.split(key, 8)
        s = 0.02
        f32 = jnp.float32
        return {'x': jax.random.normal(ks[0], (B, L, d_model), f32), 'norm_w': jnp.ones((d_model,), f32), 'in_proj_w': jax.random.normal(ks[1], (2 * d_inner, d_model), f32) * s, 'conv_w': jax.random.normal(ks[2], (d_inner, D_CONV), f32) * s, 'conv_b': jnp.zeros((d_inner,), f32), 'x_proj_w': jax.random.normal(ks[3], (dt_rank + 2 * D_STATE, d_inner), f32) * s, 'dt_proj_w': jax.random.normal(ks[4], (d_inner, dt_rank), f32) * s, 'dt_proj_b': jax.random.uniform(ks[5], (d_inner,), f32, minval=-4.0, maxval=-2.0), 'A_log': jnp.log(jnp.tile(jnp.arange(1, D_STATE + 1, dtype=f32), (d_inner, 1))), 'D': jnp.ones((d_inner,), f32), 'out_proj_w': jax.random.normal(ks[6], (d_model, d_inner), f32) * s}
    _L0_attn_in = _L0_attn_setup()

    def _L0_ffn_setup():
        import jax, jax.numpy as jnp
        import numpy as np
        D_IN, D_HID = (256, 1024)

        def _ternary(key, shape):
            return jax.random.randint(key, shape, -1, 2).astype(jnp.float32)

        def _tlin(x, w, s):
            return jnp.einsum('bsi,oi->bso', x, w) * s
        key = jax.random.key(seed)
        ks = jax.random.split(key, 12)
        inv = lambda fan: 1.0 / np.sqrt(fan).astype(np.float32)
        return {'x': jax.random.normal(ks[0], (4, 512, D_IN), dtype=jnp.float32), 'w1_w': _ternary(ks[1], (D_HID, D_IN)), 'w1_s': jax.random.uniform(ks[2], (D_HID,), dtype=jnp.float32) * inv(D_IN), 'w2_w': _ternary(ks[3], (D_HID, D_IN)), 'w2_s': jax.random.uniform(ks[4], (D_HID,), dtype=jnp.float32) * inv(D_IN), 'h1_w': _ternary(ks[5], (D_HID, D_HID)), 'h1_s': jax.random.uniform(ks[6], (D_HID,), dtype=jnp.float32) * inv(D_HID), 'h2_w': _ternary(ks[7], (D_HID, D_HID)), 'h2_s': jax.random.uniform(ks[8], (D_HID,), dtype=jnp.float32) * inv(D_HID), 'w3_w': _ternary(ks[9], (D_IN, D_HID)), 'w3_s': jax.random.uniform(ks[10], (D_IN,), dtype=jnp.float32) * inv(D_HID)}
    _L0_ffn_in = _L0_ffn_setup()
    _d = {'L0_attn_x': _L0_attn_in['x'], 'L0_attn_norm_w': _L0_attn_in['norm_w'], 'L0_attn_in_proj_w': _L0_attn_in['in_proj_w'], 'L0_attn_conv_w': _L0_attn_in['conv_w'], 'L0_attn_conv_b': _L0_attn_in['conv_b'], 'L0_attn_x_proj_w': _L0_attn_in['x_proj_w'], 'L0_attn_dt_proj_w': _L0_attn_in['dt_proj_w'], 'L0_attn_dt_proj_b': _L0_attn_in['dt_proj_b'], 'L0_attn_A_log': _L0_attn_in['A_log'], 'L0_attn_D': _L0_attn_in['D'], 'L0_attn_out_proj_w': _L0_attn_in['out_proj_w'], 'L0_ffn_w1_w': _L0_ffn_in['w1_w'], 'L0_ffn_w1_s': _L0_ffn_in['w1_s'], 'L0_ffn_w2_w': _L0_ffn_in['w2_w'], 'L0_ffn_w2_s': _L0_ffn_in['w2_s'], 'L0_ffn_h1_w': _L0_ffn_in['h1_w'], 'L0_ffn_h1_s': _L0_ffn_in['h1_s'], 'L0_ffn_h2_w': _L0_ffn_in['h2_w'], 'L0_ffn_h2_s': _L0_ffn_in['h2_s'], 'L0_ffn_w3_w': _L0_ffn_in['w3_w'], 'L0_ffn_w3_s': _L0_ffn_in['w3_s']}
    _x0 = _d['L0_attn_x']
    _d['L0_attn_x'] = jax.random.normal(jax.random.fold_in(jax.random.key(seed), 1), (2, 2048, 256), dtype=_x0.dtype)
    del _x0
    return _d

def reference(L0_attn_x, L0_attn_norm_w, L0_attn_in_proj_w, L0_attn_conv_w, L0_attn_conv_b, L0_attn_x_proj_w, L0_attn_dt_proj_w, L0_attn_dt_proj_b, L0_attn_A_log, L0_attn_D, L0_attn_out_proj_w, L0_ffn_w1_w, L0_ffn_w1_s, L0_ffn_w2_w, L0_ffn_w2_s, L0_ffn_h1_w, L0_ffn_h1_s, L0_ffn_h2_w, L0_ffn_h2_s, L0_ffn_w3_w, L0_ffn_w3_s):

    def _L0_attn_ref(x, norm_w, in_proj_w, conv_w, conv_b, x_proj_w, dt_proj_w, dt_proj_b, A_log, D, out_proj_w):
        import jax, jax.numpy as jnp
        import numpy as np
        D_MODEL = 256
        D_STATE = 16
        D_CONV = 4
        EXPAND = 2
        BATCH = 2
        SEQLEN = 512
        EPS = 1.1920928955078125e-07

        def _mamba_block(x, norm_w, in_proj_w, conv_w, conv_b, x_proj_w, dt_proj_w, dt_proj_b, A_log, D, out_proj_w):
            B, L, _ = x.shape
            d_inner, K = conv_w.shape
            dt_rank = dt_proj_w.shape[1]
            N = A_log.shape[1]
            h = x * jax.lax.rsqrt(jnp.mean(x * x, axis=-1, keepdims=True) + EPS) * norm_w
            xz = h @ in_proj_w.T
            u, z = jnp.split(xz, 2, axis=-1)
            up = jnp.pad(u, ((0, 0), (K - 1, 0), (0, 0)))
            uc = conv_b + sum((up[:, k:k + L, :] * conv_w[:, k] for k in range(K)))
            uc = jax.nn.silu(uc)
            x_dbl = uc @ x_proj_w.T
            dt, Bm, Cm = jnp.split(x_dbl, [dt_rank, dt_rank + N], axis=-1)
            dt = jax.nn.softplus(dt @ dt_proj_w.T + dt_proj_b)
            A = -jnp.exp(A_log)
            dA = jnp.exp(jnp.einsum('bld,dn->bldn', dt, A))
            dBu = jnp.einsum('bld,bln,bld->bldn', dt, Bm, uc)

            def step(hprev, inputs):
                dA_t, dBu_t, C_t = inputs
                hcur = dA_t * hprev + dBu_t
                y_t = jnp.einsum('bdn,bn->bd', hcur, C_t)
                return (hcur, y_t)
            h0 = jnp.zeros((B, d_inner, N), x.dtype)
            _, ys = jax.lax.scan(step, h0, (dA.transpose(1, 0, 2, 3), dBu.transpose(1, 0, 2, 3), Cm.transpose(1, 0, 2)))
            y = ys.transpose(1, 0, 2) + uc * D
            y = y * jax.nn.silu(z)
            out = y @ out_proj_w.T
            return out + x
        return _mamba_block(x, norm_w, in_proj_w, conv_w, conv_b, x_proj_w, dt_proj_w, dt_proj_b, A_log, D, out_proj_w)

    def _L0_ffn_ref(x, w1_w, w1_s, w2_w, w2_s, h1_w, h1_s, h2_w, h2_s, w3_w, w3_s):
        import jax, jax.numpy as jnp
        import numpy as np
        D_IN, D_HID = (256, 1024)

        def _ternary(key, shape):
            return jax.random.randint(key, shape, -1, 2).astype(jnp.float32)

        def _tlin(x, w, s):
            return jnp.einsum('bsi,oi->bso', x, w) * s
        h = jax.nn.silu(_tlin(x, w1_w, w1_s)) * _tlin(x, w2_w, w2_s)
        h = jax.nn.gelu(_tlin(h, h1_w, h1_s), approximate=False)
        h = jax.nn.gelu(_tlin(h, h2_w, h2_s), approximate=False)
        return _tlin(h, w3_w, w3_s)
    x = L0_attn_x
    x = x + _layernorm(_L0_attn_ref(_layernorm(x, axis=-1), L0_attn_norm_w, L0_attn_in_proj_w, L0_attn_conv_w, L0_attn_conv_b, L0_attn_x_proj_w, L0_attn_dt_proj_w, L0_attn_dt_proj_b, L0_attn_A_log, L0_attn_D, L0_attn_out_proj_w), axis=-1)
    x = x + _layernorm(_L0_ffn_ref(_layernorm(x, axis=-1), L0_ffn_w1_w, L0_ffn_w1_s, L0_ffn_w2_w, L0_ffn_w2_s, L0_ffn_h1_w, L0_ffn_h1_s, L0_ffn_h2_w, L0_ffn_h2_s, L0_ffn_w3_w, L0_ffn_w3_s), axis=-1)
    return x

_drawn_inputs = setup_inputs


def setup_inputs(seed=0):
    import zlib

    import numpy as np

    out = dict(_drawn_inputs(seed))
    spreads = {'L0_attn_norm_w': (1.0, 0.6), 'L0_attn_conv_b': (0.0, 0.8), 'L0_attn_D': (1.0, 0.6)}
    factors = {'L0_attn_in_proj_w': 8.0,
     'L0_attn_conv_w': 8.0,
     'L0_attn_x_proj_w': 8.0,
     'L0_attn_dt_proj_w': 8.0,
     'L0_attn_dt_proj_b': 8.0,
     'L0_attn_A_log': 8.0,
     'L0_attn_out_proj_w': 8.0}
    for name, (base, spread) in spreads.items():
        noise = np.random.default_rng([zlib.crc32(name.encode()), seed]).standard_normal(out[name].shape)
        drawn = base * np.exp(spread * noise) if base else spread * noise
        out[name] = jnp.asarray(drawn.astype(out[name].dtype))
    for name, factor in factors.items():
        out[name] = (out[name] * factor).astype(out[name].dtype)
    return out
```

```python
from contextlib import ExitStack

import concourse.bass as bass
from concourse import mybir

ALU = mybir.AluOpType
ACT = mybir.ActivationFunctionType
F32 = mybir.dt.float32
F32R = mybir.dt.float32r

P = 128
T = 256
TT = T // P
LN_EPS = 1e-5
RMS_EPS = 1.1920928955078125e-07


class Steps:

    def __init__(self, sem, names):
        self.sem, self.names = sem, list(names)
        self.per_chunk = len(self.names)

    def at(self, chunk, name):
        return chunk * self.per_chunk + (2 * self.per_chunk + self.names.index(name) + 1)


def build(nc, x, in_proj, x_proj, dt_proj, out_proj, w1, w2, h1, h2, w3, cols, w3_s, out):
    B, L, DM = x.shape
    DI = dt_proj.shape[1]
    R = dt_proj.shape[0]
    N = (x_proj.shape[1] - R) // 2
    HID = w1.shape[1]
    CONV = 4
    DT, KM, HM = DI // P, DM // P, HID // P
    CHUNKS = B * L // T
    CHUNKS_PER_SEQ = L // T
    assert CHUNKS % 2 == 0 and CHUNKS_PER_SEQ % 2 == 0 and N % 2 == 0 and DT == 4 and TT == 2

    at, col_at = 0, {}
    for name, width in (("conv_w", DT * CONV), ("conv_b", DT), ("dt_b", DT), ("D", DT), ("A_log", DT * N),
                        ("norm_w", KM), ("w1_s", HM), ("w2_s", HM), ("h1_s", HM), ("h2_s", HM)):
        col_at[name] = at
        at += width
    COLS = at

    x_in = x.rearrange("b (c t p) d -> (b c) p t d", t=TT, p=P)
    x_out = out.rearrange("b (c t p) d -> (b c) p t d", t=TT, p=P)

    ctx = ExitStack()
    with ctx:
        def sb(name, shape, dt=F32):
            return ctx.enter_context(nc.sbuf_tensor(name, shape, dt))

        def pb(name, shape):
            return ctx.enter_context(nc.psum_tensor(name, shape, F32))

        def sem(name):
            return ctx.enter_context(nc.semaphore(name))

        w_in = sb("w_in", [P, KM, 2 * DI])
        w_bc = sb("w_bc", [P, DT, 2, 2 * N])
        w_dtx = sb("w_dtx", [P, DT, R])
        w_dt = sb("w_dt", [R, DI])
        w_out = sb("w_out", [P, DT, DM])
        w_1 = sb("w_1", [P, KM, HID])
        w_2 = sb("w_2", [P, KM, HID])
        w_h1 = sb("w_h1", [P, HM, HID])
        w_h2 = sb("w_h2", [P, HM, HID])
        w_3 = sb("w_3", [P, HM, DM])
        s_3 = sb("s_3", [P, DM])
        col = sb("col", [P, COLS])
        A = sb("A", [P, DT * N])
        ident = sb("ident", [P, P])
        pick = sb("pick", [4 * N, 2 * N], F32R)

        xh = sb("xh", [P, TT, DM])
        u_ext = sb("u_ext", [P, DT, CONV - 1 + T])
        uc = [sb(f"uc{i}", [P, DT, T]) for i in range(2)]
        z = [sb(f"z{i}", [P, DT, T]) for i in range(2)]
        delta = [sb(f"delta{i}", [P, DT, T]) for i in range(2)]
        X = [sb(f"X{i}", [P, DT, T]) for i in range(2)]
        BC = [sb(f"BC{i}", [4 * N, T], F32R) for i in range(2)]
        dtx = sb("dtx", [R, T])
        e_sp = sb("e_sp", [P, DT, T])
        hn = e_sp[:, 0:2, :].rearrange("p t (a d) -> p (t a) d", d=DM)
        hT = e_sp[:, 2:4, :]
        t_sp = sb("t_sp", [P, DT, T])
        hstat = sb("hstat", [P, TT, 6])
        hmv = sb("hmv", [P, TT, 2])
        hsm = sb("hsm", [P, 16, TT])

        dA = [sb(f"dA{i}", [P, DT, T]) for i in range(2)]
        Bs = [sb(f"Bs{i}", [P, T]) for i in range(2)]
        S = [sb(f"S{i}", [P, DT, T]) for i in range(3)]
        gate = sb("gate", [P, 1])
        carry = sb("carry", [P, N, DT])

        xt = sb("xt", [P, TT, DM])
        o = sb("o", [P, TT, DM])
        x1 = sb("x1", [P, TT, DM])
        xf = sb("xf", [P, TT, DM])
        xfT = sb("xfT", [P, KM, T])
        Rw = sb("Rw", [P, HM, T])
        G = sb("G", [P, HM, T])
        fo = o
        ob = sb("ob", [P, TT, DM])
        mr = [sb(f"mr{i}", [P, 2, TT]) for i in range(2)]
        tstat = sb("tstat", [P, TT, 6])
        tmv = sb("tmv", [P, TT, 2])
        tsm = sb("tsm", [P, 16, TT])

        yP = pb("yP", [P, DT, T])
        bP = [pb(f"bP{i}", [P, 2, T]) for i in range(2)]
        hP = [pb(f"hP{i}", [P, 2, T]) for i in range(2)]
        fP = [pb(f"fP{i}", [P, 2, T]) for i in range(2)]

        def c_(name, i, n=1):
            return col[:, col_at[name] + i:col_at[name] + i + n]

        HV = Steps(sem("head_vector"),
                   ["x_stats", "x_aggr", "w", "n1", "n2", "n3", "r1", "q1", "q2", "w2", "nmr1",
                    "m1", "m2", "m3", "r2", "r12", "nmr12", "halo", "tap0", "tap1", "tap2",
                    "bc_hi", "bc_lo", "t1"])
        SV = Steps(sem("scan_vector"),
                   [f"{k}{n}" for n in range(N) for k in ("s0_", "s1_", "s2_", "s3_", "carry", "g")])
        TV = Steps(sem("tail_vector"),
                   ["y_d", "yz", "o_mul", "o_add", "o_stats", "o_aggr", "o_w", "o_n1", "o_n2", "o_n3", "o_r",
                    "o_nmr", "x1", "x_stats", "x_aggr", "x_w", "x_n1", "x_n2", "x_n3", "x_r", "x_nmr"]
                   + [f"b{m}" for m in range(HM)]
                   + ["f_out", "f_stats", "f_aggr", "f_w", "f_n1", "f_n2", "f_n3", "f_r", "f_nmr", "out_add"])
        HA = Steps(sem("head_scalar"),
                   ["ln1", "ex1", "ln2", "ex2", "hn", "hT", "u0", "u1", "cbase", "silu_u", "z0", "z1",
                    "dtx", "v0", "v1", "e", "l"])
        SA = Steps(sem("scan_scalar"),
                   [f"{k}{n}" for n in range(N) for k in ("b", "e0_", "e1_", "e2_", "e3_")])
        TA = Steps(sem("tail_scalar"),
                   ["o_ln", "o_ex", "o_norm", "x_ln", "x_ex", "xf", "xfT"] + [f"a{m}" for m in range(HM)]
                   + ["silu"] + [f"h1_{i}" for i in range(HM // 2)] + ["gelu1"]
                   + [f"h2_{i}" for i in range(HM // 2)] + ["gelu2", "f_ln", "f_ex", "f_norm"])
        HP = Steps(sem("head_tensor"), ["hT", "u0", "u1", "z0", "z1", "xp", "d0", "d1"])
        SB = Steps(sem("scan_tensor_bcast"), [f"b{n}" for n in range(N)])
        SY = Steps(sem("scan_tensor_sum"), [f"y{n}" for n in range(N)])
        TP = Steps(sem("tail_tensor"),
                   ["out", "xfT"] + [f"ab{m}" for m in range(HM)] + [f"h1_{i}" for i in range(HM // 2)]
                   + [f"h2_{i}" for i in range(HM // 2)] + ["w3"])
        HL = Steps(sem("head_pool"), ["res", "log1p", "delta", "X"])
        SL = Steps(sem("scan_pool"), [f"dBu{n}" for n in range(N)])
        TL = Steps(sem("tail_pool"), ["G"])
        xh_loaded = Steps(sem("xh_loaded"), ["dma"] * 15 + ["landed"])
        xt_loaded = Steps(sem("xt_loaded"), ["dma"] * 15 + ["landed"])
        out_stored = Steps(sem("out_stored"), ["dma"] * 15 + ["landed"])
        weights_in = sem("weights_in")
        ident_made = sem("ident_made")
        pick_made = sem("pick_made")
        A_made = sem("A_made")
        carry_clear = sem("carry_clear")

        def start(eng, *steps):
            for s in steps:
                eng.sem_inc(s.sem, 2 * s.per_chunk)

        n_weights = [0]

        def load(eng, dst, src):
            eng.dma_start(dst, src).then_inc(weights_in, 16)
            n_weights[0] += 1

        WEIGHTS = 15

        def iterate(body, engine):
            body(-1, 1, head=True)
            body(0, 0, scan=True, head=True)
            with engine.Fori(0, (CHUNKS - 2) // 2) as j:
                body(j * 2 + 1, 1, scan=True, head=True, tail=True, j=j)
                body(j * 2 + 2, 0, scan=True, head=True, tail=True, j=j)
            body(CHUNKS - 1, 1, scan=True, tail=True)
            body(CHUNKS, 0, tail=True)

        SLOTS = N

        def slot(par, n):
            return (n + par) % 3

        def slot_before(c, par, n):
            for m in range(n - 1, -1, -1):
                if slot(par, m) == slot(par, n):
                    return c, f"y{m}"
            for m in range(N - 1, -1, -1):
                if slot(1 - par, m) == slot(par, n):
                    return c - 1, f"y{m}"

        block = ctx.enter_context(nc.Block())

        @block.sync
        def _(sp):
            start(sp, xh_loaded, xt_loaded, out_stored)
            sp.dma_start(xh[:, :, :], x_in[0]).then_inc(xh_loaded.sem, 16)
            load(sp, col[:, :], cols)
            load(sp, w_in[:, :, :], in_proj.rearrange("(k p) n -> p k n", p=P))
            xp = x_proj.rearrange("(k p) n -> p k n", p=P)
            load(sp, w_dtx[:, :, :], xp[:, :, 0:R])
            load(sp, w_bc[:, :, 0, :], xp[:, :, R:R + 2 * N])
            load(sp, w_bc[:, :, 1, :], xp[:, :, R:R + 2 * N])
            load(sp, w_dt[:, :], dt_proj)
            load(sp, w_out[:, :, :], out_proj.rearrange("(k p) n -> p k n", p=P))
            load(sp, w_1[:, :, :], w1.rearrange("(k p) n -> p k n", p=P))
            load(sp, w_2[:, :, :], w2.rearrange("(k p) n -> p k n", p=P))
            for i in range(2):
                half = slice(i * HM // 2, (i + 1) * HM // 2)
                load(sp, w_h1[:, half, :], h1.rearrange("(k p) n -> p k n", p=P)[:, half, :])
                load(sp, w_h2[:, half, :], h2.rearrange("(k p) n -> p k n", p=P)[:, half, :])
            load(sp, w_3[:, :, :], w3.rearrange("(k p) n -> p k n", p=P))
            load(sp, s_3[:, :], w3_s.partition_broadcast(P))
            assert n_weights[0] == WEIGHTS

            def chunk(c, more, before):
                if more:
                    sp.wait_ge(HA.sem, HA.at(c, "hn"))
                    sp.dma_start(xh[:, :, :], x_in[c + 1]).then_inc(xh_loaded.sem, 16)
                if before is not None:
                    sp.wait_ge(TV.sem, TV.at(before, "x1"))
                sp.dma_start(xt[:, :, :], x_in[c]).then_inc(xt_loaded.sem, 16)
                if before is not None:
                    sp.wait_ge(TV.sem, TV.at(before, "out_add"))
                    sp.dma_start(x_out[before], ob[:, :, :]).then_inc(out_stored.sem, 16)

            chunk(0, True, None)
            with sp.Fori(1, CHUNKS - 1) as c:
                chunk(c, True, c - 1)
            chunk(CHUNKS - 1, False, CHUNKS - 2)
            sp.wait_ge(TV.sem, TV.at(CHUNKS - 1, "out_add"))
            sp.dma_start(x_out[CHUNKS - 1], ob[:, :, :]).then_inc(out_stored.sem, 16)
            sp.wait_ge(out_stored.sem, out_stored.at(CHUNKS - 1, "landed"))

        @block.gpsimd
        def _(pool):
            start(pool, HL, SL, TL)
            pool.memset(ident[:, :], 0.0).then_inc(ident_made, 1)
            pool.wait_ge(ident_made, 1)
            pool.affine_select(out=ident[:, :], in_=ident[:, :], compare_op=ALU.not_equal, fill=1.0,
                               base=0, pattern=[[-1, P]], channel_multiplier=1).then_inc(ident_made, 1)

            def front(c, par, n):
                pool.wait_ge(SA.sem, SA.at(c, f"b{n}"))
                if n == 0:
                    pool.wait_ge(HL.sem, HL.at(c, "X"))
                k = slot(par, n)
                before, read = slot_before(c, par, n)
                pool.wait_ge(SY.sem, SY.at(before, read))
                pool.tensor_tensor(S[k][:, :, :], X[par][:, :, :],
                                   Bs[n % 2][:, None, :].broadcast_to([P, DT, T]), ALU.mult).then_inc(SL.sem, 1)

            def body(c, par, scan=False, head=False, tail=False, j=None):
                for n in range(SLOTS):
                    if scan and n + 1 < N:
                        front(c, par, n + 1)
                    if n == N - 1 and head:
                        front(c + 1, 1 - par, 0)
                    if n == 7 and tail:
                        pool.wait_ge(TA.sem, TA.at(c - 1, "silu"))
                        pool.wait_ge(TV.sem, TV.at(c - 1, f"b{HM - 1}"))
                        pool.tensor_tensor(G[:, :, :], Rw[:, :, :], G[:, :, :], ALU.mult).then_inc(TL.sem, 1)
                    if n == 9 and head:
                        h, hp = c + 1, 1 - par
                        pool.wait_ge(HV.sem, HV.at(h, "t1"))
                        pool.tensor_tensor(t_sp[:, :, :], e_sp[:, :, :], t_sp[:, :, :],
                                           ALU.subtract).then_inc(HL.sem, 1)
                        pool.wait_ge(HL.sem, HL.at(h, "res"))
                        pool.wait_ge(HA.sem, HA.at(h, "l"))
                        pool.tensor_tensor(X[hp][:, :, :], X[hp][:, :, :], t_sp[:, :, :], ALU.add).then_inc(HL.sem, 1)
                        pool.wait_ge(HL.sem, HL.at(h, "log1p"))
                        pool.tensor_tensor(delta[hp][:, :, :], delta[hp][:, :, :], X[hp][:, :, :],
                                           ALU.add).then_inc(HL.sem, 1)
                        pool.wait_ge(HL.sem, HL.at(h, "delta"))
                        pool.tensor_tensor(X[hp][:, :, :], delta[hp][:, :, :], uc[hp][:, :, :],
                                           ALU.mult).then_inc(HL.sem, 1)

            iterate(body, pool)

        @block.tensor
        def _(pe):
            start(pe, HP, SB, SY, TP)
            pe.wait_ge(ident_made, 2)
            pe.wait_ge(weights_in, 16 * WEIGHTS)
            pe.wait_ge(pick_made, 1)

            def products(dst, lhs, rhs, k):
                for i in range(k):
                    mm = pe.matmul(dst, lhs(i), rhs(i), start=(i == 0), stop=(i == k - 1))
                return mm

            def bcast(c, par, n):
                if n == 0:
                    pe.wait_ge(HV.sem, HV.at(c, "bc_lo"))
                if n >= 2:
                    pe.wait_ge(SV.sem, SV.at(c, f"g{n - 2}"))
                else:
                    pe.wait_ge(SV.sem, SV.at(c - 1, f"g{N - 2 + n}"))
                for i, r in ((0, n), (1, N + n)):
                    mm = pe.matmul(bP[n % 2][:, i, :], pick[:, r:r + 1].broadcast_to([4 * N, P]), BC[par][:, :],
                                   start=True, stop=True)
                mm.then_inc(SB.sem, 1)

            def state_sum(c, par, n):
                pe.wait_ge(SV.sem, SV.at(c, f"g{n}"))
                if n == 0:
                    pe.wait_ge(TV.sem, TV.at(c - 1, "y_d"))
                k = slot(par, n)
                for i in range(DT // 2):
                    mm = pe.matmul(yP[:, 2 * i:2 * i + 2, :], ident[:, :], S[k][:, 2 * i:2 * i + 2, :],
                                   start=(n == 0), stop=(n == N - 1))
                mm.then_inc(SY.sem, 1)

            def head_step(h, hp, n):
                if n == 4:
                    pe.wait_ge(HA.sem, HA.at(h, "hn"))
                    pe.wait_ge(HA.sem, HA.at(h - 1, "v0"))
                    for k in range(KM):
                        for t in range(TT):
                            mm = pe.transpose(hP[0][:, k, t * P:(t + 1) * P], hn[:, t, k * P:(k + 1) * P], ident[:, :])
                    mm.then_inc(HP.sem, 1)
                if n in (5, 6):
                    if n == 5:
                        pe.wait_ge(HA.sem, HA.at(h, "hT"))
                    for i in range(2):
                        q = 2 * (n - 5) + i
                        if q == 0:
                            pe.wait_ge(HA.sem, HA.at(h - 1, "v1"))
                        else:
                            pe.wait_ge(HA.sem, HA.at(h, ("hT", "u0", "u1")[q - 1]))
                        for d in range(2):
                            mm = products(hP[(q + 1) % 2][:, d, :],
                                          lambda k: w_in[:, k, (2 * q + d) * P:(2 * q + d + 1) * P],
                                          lambda k: hT[:, k, :], KM)
                        mm.then_inc(HP.sem, 1)
                if n == 8:
                    pe.wait_ge(HA.sem, HA.at(h, "silu_u"))
                    pe.wait_ge(HA.sem, HA.at(h, "z0"))
                    products(hP[1][0:4 * N, 0, :], lambda k: w_bc[:, k, :, :].rearrange("p a n -> p (a n)"),
                             lambda k: uc[hp][:, k, :], DT)
                    products(hP[1][0:R, 1, :], lambda k: w_dtx[:, k, :],
                             lambda k: uc[hp][:, k, :], DT).then_inc(HP.sem, 1)
                    pe.wait_ge(HA.sem, HA.at(h, "dtx"))
                    pe.wait_ge(HA.sem, HA.at(h, "z1"))
                    for q in range(2):
                        if q == 1:
                            pe.wait_ge(HV.sem, HV.at(h, "bc_lo"))
                        for d in range(2):
                            m = 2 * q + d
                            mm = pe.matmul(hP[q][:, d, :], w_dt[:, m * P:(m + 1) * P], dtx[:, :],
                                           start=True, stop=True)
                        mm.then_inc(HP.sem, 1)

            def tail_step(f, fp, n):
                def bank(k):
                    return fP[(fp + k) % 2]
                if n == 0:
                    pe.wait_ge(TV.sem, TV.at(f, "yz"))
                    pe.wait_ge(TA.sem, TA.at(f - 1, f"h2_{HM // 2 - 1}"))
                    for t in range(TT):
                        mm = products(bank(0)[:, t, :], lambda k: z[fp][:, k, t * P:(t + 1) * P],
                                      lambda k: w_out[:, k, :], DT)
                    mm.then_inc(TP.sem, 1)
                if n == 5:
                    pe.wait_ge(TA.sem, TA.at(f, "xf"))
                    pe.wait_ge(TV.sem, TV.at(f - 1, "f_out"))
                    for k in range(KM):
                        for t in range(TT):
                            mm = pe.transpose(bank(1)[:, k, t * P:(t + 1) * P], xf[:, t, k * P:(k + 1) * P], ident[:, :])
                    mm.then_inc(TP.sem, 1)
                if n in (6, 7):
                    if n == 6:
                        pe.wait_ge(TA.sem, TA.at(f, "xfT"))
                    for m in range(4 * (n - 6), 4 * (n - 5)):
                        if m == 0:
                            pe.wait_ge(TV.sem, TV.at(f, "o_mul"))
                        if m >= 2:
                            pe.wait_ge(TA.sem, TA.at(f, f"a{m - 2}"))
                            pe.wait_ge(TV.sem, TV.at(f, f"b{m - 2}"))
                        for i, w in enumerate((w_1, w_2)):
                            mm = products(bank(2 + m)[:, i, :], lambda k: w[:, k, m * P:(m + 1) * P],
                                          lambda k: xfT[:, k, :], KM)
                        mm.then_inc(TP.sem, 1)
                for s, w, first, src in ((8, w_h1, "h1", "G"), (11, w_h2, "h2", "gelu1")):
                    if s <= n < s + 3:
                        for i in ((0, 1), (2,), (3,))[n - s]:
                            if i == 0:
                                if first == "h1":
                                    pe.wait_ge(TL.sem, TL.at(f, "G"))
                                    pe.wait_ge(TA.sem, TA.at(f, f"a{HM - 2}"))
                                    pe.wait_ge(TV.sem, TV.at(f, f"b{HM - 2}"))
                                else:
                                    pe.wait_ge(TA.sem, TA.at(f, "gelu1"))
                            elif i == 1:
                                if first == "h1":
                                    pe.wait_ge(TA.sem, TA.at(f, f"a{HM - 1}"))
                                    pe.wait_ge(TV.sem, TV.at(f, f"b{HM - 1}"))
                                else:
                                    pe.wait_ge(TA.sem, TA.at(f, "h1_3"))
                            else:
                                pe.wait_ge(TA.sem, TA.at(f, f"{first}_{i - 2}"))
                            k0 = (10 if first == "h1" else 14) + i
                            for d in range(2):
                                m = 2 * i + d
                                mm = products(bank(k0)[:, d, :], lambda k: w[:, k, m * P:(m + 1) * P],
                                              lambda k: G[:, k, :], HM)
                            mm.then_inc(TP.sem, 1)
                if n == 14:
                    pe.wait_ge(TA.sem, TA.at(f, "gelu2"))
                    for t in range(TT):
                        mm = products(bank(18)[:, t, :], lambda k: G[:, k, t * P:(t + 1) * P],
                                      lambda k: w_3[:, k, :], HM)
                    mm.then_inc(TP.sem, 1)

            def body(c, par, scan=False, head=False, tail=False, j=None):
                for n in range(SLOTS):
                    if scan and n + 1 < N:
                        bcast(c, par, n + 1)
                    if n == N - 1 and head:
                        bcast(c + 1, 1 - par, 0)
                    if tail:
                        tail_step(c - 1, 1 - par, n)
                    if head:
                        head_step(c + 1, 1 - par, n)
                    if scan:
                        state_sum(c, par, n)

            iterate(body, pe)

        @block.scalar
        def _(act):
            start(act, HA, SA, TA)
            act.wait_ge(weights_in, 16 * WEIGHTS)
            act.preload_act_table_set("natural_log_exp_and_others")
            act.activation(A[:, :], c_("A_log", 0, DT * N), ACT.Exp).then_inc(A_made, 1)
            act.wait_ge(A_made, 1)
            act.mul(A[:, :], A[:, :], -1.0).then_inc(A_made, 1)
            act.wait_ge(A_made, 2)

            def front(c, par, n):
                act.wait_ge(SB.sem, SB.at(c, f"b{n}"))
                if n >= 2:
                    act.wait_ge(SL.sem, SL.at(c, f"dBu{n - 2}"))
                else:
                    act.wait_ge(SL.sem, SL.at(c - 1, f"dBu{N - 2 + n}"))
                act.copy(Bs[n % 2][:, :], bP[n % 2][:, 0, :]).then_inc(SA.sem, 1)
                if n == 0:
                    act.wait_ge(HL.sem, HL.at(c, "delta"))
                for d in range(DT):
                    if n >= 2:
                        act.wait_ge(SV.sem, SV.at(c, f"s{d}_{n - 2}"))
                    else:
                        act.wait_ge(SV.sem, SV.at(c - 1, f"s{d}_{N - 2 + n}"))
                    act.activation(dA[n % 2][:, d, :], delta[par][:, d, :], ACT.Exp,
                                   scale=A[:, d * N + n:d * N + n + 1]).then_inc(SA.sem, 1)

            def rsqrt_guess(steps, vsteps, c, sm, names, w, src):
                act.wait_ge(vsteps.sem, vsteps.at(c, w))
                act.activation(sm[:, src + 1, :], sm[:, src, :], ACT.Ln).then_inc(steps.sem, 1)
                act.wait_ge(steps.sem, steps.at(c, names[0]))
                act.activation(sm[:, src + 2, :], sm[:, src + 1, :], ACT.Exp, scale=-0.5).then_inc(steps.sem, 1)

            def head_step(h, hp, n):
                if n == 1:
                    rsqrt_guess(HA, HV, h, hsm, ("ln1", "ex1"), "w", 0)
                if n == 2:
                    rsqrt_guess(HA, HV, h, hsm, ("ln2", "ex2"), "w2", 6)
                if n == 3:
                    act.wait_ge(HV.sem, HV.at(h, "nmr12"))
                    act.wait_ge(HL.sem, HL.at(h - 1, "res"))
                    for t in range(TT):
                        a = act.activation(hn[:, t, :], xh[:, t, :], ACT.Identity,
                                           scale=hsm[:, 12, t:t + 1], bias=hsm[:, 13, t:t + 1])
                    a.then_inc(HA.sem, 1)
                if n == 4:
                    act.wait_ge(HP.sem, HP.at(h, "hT"))
                    act.wait_ge(HP.sem, HP.at(h - 1, "z1"))
                    for k in range(KM):
                        a = act.activation(hT[:, k, :], hP[0][:, k, :], ACT.Copy, scale=c_("norm_w", k))
                    a.then_inc(HA.sem, 1)
                if n == 5:
                    act.wait_ge(HV.sem, HV.at(h, "halo"))
                    for q in range(2):
                        act.wait_ge(HP.sem, HP.at(h, f"u{q}"))
                        act.copy(u_ext[:, 2 * q:2 * q + 2, CONV - 1:], hP[(q + 1) % 2][:, :, :]).then_inc(HA.sem, 1)
                    act.wait_ge(HA.sem, HA.at(h, "u1"))
                    act.wait_ge(TP.sem, TP.at(h - 2, "out"))
                    for d in range(DT):
                        a = act.activation(uc[hp][:, d, :], u_ext[:, d, CONV - 1:], ACT.Identity,
                                           scale=c_("conv_w", d * CONV + CONV - 1), bias=c_("conv_b", d))
                    a.then_inc(HA.sem, 1)
                if n == 7:
                    act.wait_ge(HV.sem, HV.at(h, "tap2"))
                    act.activation(uc[hp][:, :, :], uc[hp][:, :, :], ACT.Silu).then_inc(HA.sem, 1)
                    for q in range(2):
                        act.wait_ge(HP.sem, HP.at(h, f"z{q}"))
                        act.activation(z[hp][:, 2 * q:2 * q + 2, :], hP[(q + 1) % 2][:, :, :],
                                       ACT.Silu).then_inc(HA.sem, 1)
                if n == 8:
                    act.wait_ge(HP.sem, HP.at(h, "xp"))
                    act.wait_ge(HP.sem, HP.at(h - 1, "d1"))
                    act.copy(dtx[:, :], hP[1][0:R, 1, :]).then_inc(HA.sem, 1)
                if n == 9:
                    act.wait_ge(HL.sem, HL.at(h - 1, "log1p"))
                    act.wait_ge(SL.sem, SL.at(h - 2, f"dBu{N - 1}"))
                    for q in range(2):
                        act.wait_ge(HP.sem, HP.at(h, f"d{q}"))
                        for i in range(2):
                            d = 2 * q + i
                            act.activation(e_sp[:, d, :], hP[q][:, i, :], ACT.Abs, bias=c_("dt_b", d))
                            a = act.activation(delta[hp][:, d, :], hP[q][:, i, :], ACT.Relu, bias=c_("dt_b", d))
                        a.then_inc(HA.sem, 1)
                    act.wait_ge(HA.sem, HA.at(h, "v1"))
                    act.activation(e_sp[:, :, :], e_sp[:, :, :], ACT.Exp, scale=-1.0).then_inc(HA.sem, 1)
                    act.wait_ge(HA.sem, HA.at(h, "e"))
                    act.activation(X[hp][:, :, :], e_sp[:, :, :], ACT.Ln, bias=1.0).then_inc(HA.sem, 1)

            def tail_step(f, fp, n):
                def bank(k):
                    return fP[(fp + k) % 2]
                if n == 1:
                    rsqrt_guess(TA, TV, f, tsm, ("o_ln", "o_ex"), "o_w", 0)
                if n == 2:
                    act.wait_ge(TV.sem, TV.at(f, "o_nmr"))
                    for t in range(TT):
                        a = act.activation(o[:, t, :], o[:, t, :], ACT.Identity,
                                           scale=tsm[:, 3, t:t + 1], bias=tsm[:, 4, t:t + 1])
                    a.then_inc(TA.sem, 1)
                if n == 3:
                    rsqrt_guess(TA, TV, f, tsm, ("x_ln", "x_ex"), "x_w", 5)
                if n == 4:
                    act.wait_ge(TV.sem, TV.at(f, "x_nmr"))
                    act.wait_ge(TP.sem, TP.at(f - 1, "xfT"))
                    for t in range(TT):
                        a = act.activation(xf[:, t, :], x1[:, t, :], ACT.Identity,
                                           scale=tsm[:, 8, t:t + 1], bias=tsm[:, 9, t:t + 1])
                    a.then_inc(TA.sem, 1)
                if n == 5:
                    act.wait_ge(TP.sem, TP.at(f, "xfT"))
                    act.copy(xfT[:, :, :], bank(1)[:, :, :]).then_inc(TA.sem, 1)
                if n in (6, 7):
                    for m in range(4 * (n - 6), 4 * (n - 5)):
                        act.wait_ge(TP.sem, TP.at(f, f"ab{m}"))
                        act.activation(Rw[:, m, :], bank(2 + m)[:, 0, :], ACT.Copy,
                                       scale=c_("w1_s", m)).then_inc(TA.sem, 1)
                if n == 7:
                    act.wait_ge(TA.sem, TA.at(f, f"a{HM - 1}"))
                    act.activation(Rw[:, :, :], Rw[:, :, :], ACT.Silu).then_inc(TA.sem, 1)
                for s, name, gelu in ((8, "h1", "gelu1"), (11, "h2", "gelu2")):
                    if s <= n < s + 3:
                        for i in ((0, 1), (2,), (3,))[n - s]:
                            if i == 0 and name == "h1":
                                act.wait_ge(TL.sem, TL.at(f, "G"))
                            act.wait_ge(TP.sem, TP.at(f, f"{name}_{i}"))
                            for d in range(2):
                                m = 2 * i + d
                                a = act.activation(Rw[:, m, :], bank((10 if name == "h1" else 14) + i)[:, d, :],
                                                   ACT.Copy, scale=c_(f"{name}_s", m))
                            a.then_inc(TA.sem, 1)
                    if n == s + 2:
                        act.wait_ge(TA.sem, TA.at(f, f"{name}_3"))
                        act.activation(G[:, :, :], Rw[:, :, :], ACT.Gelu).then_inc(TA.sem, 1)
                        act.preload_act_table_set("natural_log_exp_and_others")
                if n == 15:
                    rsqrt_guess(TA, TV, f, tsm, ("f_ln", "f_ex"), "f_w", 10)
                    act.wait_ge(TV.sem, TV.at(f, "f_nmr"))
                    for t in range(TT):
                        a = act.activation(fo[:, t, :], fo[:, t, :], ACT.Identity,
                                           scale=tsm[:, 13, t:t + 1], bias=tsm[:, 14, t:t + 1])
                    a.then_inc(TA.sem, 1)

            def body(c, par, scan=False, head=False, tail=False, j=None):
                for n in range(SLOTS):
                    if scan and n + 1 < N:
                        front(c, par, n + 1)
                    if n == N - 1 and head:
                        front(c + 1, 1 - par, 0)
                    if n == 7:
                        if tail:
                            tail_step(c - 1, 1 - par, n)
                        if head:
                            head_step(c + 1, 1 - par, n)
                        act.preload_act_table_set("natural_log_exp_and_others")
                        continue
                    if tail:
                        tail_step(c - 1, 1 - par, n)
                    if head:
                        head_step(c + 1, 1 - par, n)

            iterate(body, act)

        @block.vector
        def _(dve):
            start(dve, HV, SV, TV)
            dve.memset(carry[:, :, :], 0.0).then_inc(carry_clear, 1)
            dve.wait_ge(carry_clear, 1)
            dve.wait_ge(ident_made, 2)
            dve.tensor_tensor(pick[:, :], ident[0:4 * N, 0:2 * N], ident[0:4 * N, 2 * N:4 * N],
                              ALU.add).then_inc(pick_made, 1)
            dve.wait_ge(weights_in, 16 * WEIGHTS)

            def newton(steps, c, names, sm, src, y):
                w, l, g = sm[:, src, :], sm[:, src + 1, :], sm[:, src + 2, :]
                dve.tensor_tensor(l, g, g, ALU.mult).then_inc(steps.sem, 1)
                dve.wait_ge(steps.sem, steps.at(c, names[0]))
                dve.tensor_tensor(l, l, w, ALU.mult).then_inc(steps.sem, 1)
                dve.wait_ge(steps.sem, steps.at(c, names[1]))
                dve.tensor_scalar(l, l, -0.5, 1.5, ALU.mult, ALU.add).then_inc(steps.sem, 1)
                dve.wait_ge(steps.sem, steps.at(c, names[2]))
                dve.tensor_tensor(y, g, l, ALU.mult).then_inc(steps.sem, 1)
                dve.wait_ge(steps.sem, steps.at(c, names[3]))

            def stats(steps, c, names, src, stat, mv):
                for t in range(TT):
                    a = dve.bn_stats(stat[:, t, :], src[:, t, :])
                a.then_inc(steps.sem, 1)
                dve.wait_ge(steps.sem, steps.at(c, names[0]))
                dve.memset(gate[:, :], 0.0)
                for t in range(TT):
                    a = dve.bn_aggr(mv[:, t, :], stat[:, t, :])
                a.then_inc(steps.sem, 1)
                dve.wait_ge(steps.sem, steps.at(c, names[1]))

            def minus_mean(steps, c, name, dst, mv, r, wait_for=True):
                dve.scalar_tensor_tensor(dst, mv[:, :, 0], -1.0, r, ALU.mult, ALU.mult).then_inc(steps.sem, 1)
                if wait_for:
                    dve.wait_ge(steps.sem, steps.at(c, name))

            def back(c, par, n):
                k = slot(par, n)
                dve.wait_ge(SL.sem, SL.at(c, f"dBu{n}"))
                for d in range(DT):
                    dve.wait_ge(SA.sem, SA.at(c, f"e{d}_{n}"))
                    dve.tensor_tensor_scan(S[k][:, d, :], dA[n % 2][:, d, :], S[k][:, d, :],
                                           carry[:, n, d:d + 1], ALU.mult, ALU.add).then_inc(SV.sem, 1)
                dve.wait_ge(SV.sem, SV.at(c, f"s{DT - 1}_{n}"))
                dve.tensor_copy(carry[:, n, :], S[k][:, :, T - 1]).then_inc(SV.sem, 1)
                dve.wait_ge(SV.sem, SV.at(c, f"carry{n}"))
                dve.wait_ge(SB.sem, SB.at(c, f"b{n}"))
                dve.tensor_tensor(S[k][:, :, :], S[k][:, :, :],
                                  bP[n % 2][:, 1:2, :].broadcast_to([P, DT, T]), ALU.mult).then_inc(SV.sem, 1)

            def head_step(h, hp, n, j, first):
                if n == 1:
                    dve.wait_ge(xh_loaded.sem, xh_loaded.at(h, "landed"))
                    stats(HV, h, ("x_stats", "x_aggr"), xh, hstat, hmv)
                    dve.tensor_scalar(hsm[:, 0, :], hmv[:, :, 1], LN_EPS, None, ALU.add).then_inc(HV.sem, 1)
                if n == 2:
                    r1 = mr[hp][:, 0, :]
                    dve.wait_ge(HA.sem, HA.at(h, "ex1"))
                    newton(HV, h, ("n1", "n2", "n3", "r1"), hsm, 0, r1)
                    dve.tensor_tensor(hsm[:, 5, :], r1, r1, ALU.mult).then_inc(HV.sem, 1)
                    dve.wait_ge(HV.sem, HV.at(h, "q1"))
                    dve.tensor_tensor(hsm[:, 5, :], hsm[:, 5, :], hmv[:, :, 1], ALU.mult).then_inc(HV.sem, 1)
                    dve.wait_ge(HV.sem, HV.at(h, "q2"))
                    dve.tensor_scalar(hsm[:, 6, :], hsm[:, 5, :], RMS_EPS, None, ALU.add).then_inc(HV.sem, 1)
                    dve.wait_ge(HV.sem, HV.at(h, "w2"))
                    minus_mean(HV, h, "nmr1", mr[hp][:, 1, :], hmv, r1)
                if n == 3:
                    dve.wait_ge(HA.sem, HA.at(h, "ex2"))
                    newton(HV, h, ("m1", "m2", "m3", "r2"), hsm, 6, hsm[:, 9, :])
                    dve.tensor_tensor(hsm[:, 12, :], mr[hp][:, 0, :], hsm[:, 9, :], ALU.mult).then_inc(HV.sem, 1)
                    dve.wait_ge(HV.sem, HV.at(h, "r12"))
                    minus_mean(HV, h, "nmr12", hsm[:, 13, :], hmv, hsm[:, 12, :], False)
                if n == 4:
                    ahead, last = u_ext[:, :, 0:CONV - 1], u_ext[:, :, T:T + CONV - 1]
                    if first is True:
                        dve.memset(ahead, 0.0).then_inc(HV.sem, 1)
                    elif first is None:
                        dve.tensor_copy(ahead, last).then_inc(HV.sem, 1)
                    else:
                        with dve.If(first):
                            dve.memset(ahead, 0.0).then_inc(HV.sem, 1)
                        with dve.Else():
                            dve.tensor_copy(ahead, last).then_inc(HV.sem, 1)
                if n == 6:
                    dve.wait_ge(HA.sem, HA.at(h, "cbase"))
                    for k in range(CONV - 1):
                        for d in range(DT):
                            a = dve.scalar_tensor_tensor(uc[hp][:, d, :], u_ext[:, d, k:k + T],
                                                         c_("conv_w", d * CONV + k), uc[hp][:, d, :],
                                                         ALU.mult, ALU.add)
                        a.then_inc(HV.sem, 1)
                        dve.wait_ge(HV.sem, HV.at(h, f"tap{k}"))
                if n == 8:
                    dve.wait_ge(HA.sem, HA.at(h, "dtx"))
                    dve.tensor_copy(BC[hp][:, :], hP[1][0:4 * N, 0, :]).then_inc(HV.sem, 1)
                    dve.wait_ge(HV.sem, HV.at(h, "bc_hi"))
                    lo = slice(2 * N, 4 * N)
                    dve.tensor_tensor(BC[hp][lo, :], hP[1][lo, 0, :], BC[hp][lo, :].bitcast(F32), ALU.subtract).then_inc(HV.sem, 1)
                if n == 9:
                    dve.wait_ge(HA.sem, HA.at(h, "e"))
                    dve.tensor_scalar(t_sp[:, :, :], e_sp[:, :, :], 1.0, -1.0, ALU.add, ALU.add).then_inc(HV.sem, 1)

            def tail_step(f, fp, n):
                def bank(k):
                    return fP[(fp + k) % 2]
                if n == 0:
                    dve.wait_ge(SY.sem, SY.at(f, f"y{N - 1}"))
                    for d in range(DT):
                        a = dve.scalar_tensor_tensor(uc[fp][:, d, :], uc[fp][:, d, :], c_("D", d), yP[:, d, :],
                                                     ALU.mult, ALU.add)
                    a.then_inc(TV.sem, 1)
                    dve.wait_ge(TV.sem, TV.at(f, "y_d"))
                    dve.tensor_tensor(z[fp][:, :, :], uc[fp][:, :, :], z[fp][:, :, :], ALU.mult).then_inc(TV.sem, 1)
                if n == 1:
                    dve.wait_ge(xt_loaded.sem, xt_loaded.at(f, "landed"))
                    dve.wait_ge(TP.sem, TP.at(f, "out"))
                    for t in range(TT):
                        a = dve.scalar_tensor_tensor(o[:, t, :], xt[:, t, :], mr[fp][:, 0, t:t + 1], bank(0)[:, t, :],
                                                     ALU.mult, ALU.add)
                    a.then_inc(TV.sem, 1)
                    dve.wait_ge(TV.sem, TV.at(f, "o_mul"))
                    for t in range(TT):
                        a = dve.tensor_scalar(o[:, t, :], o[:, t, :], mr[fp][:, 1, t:t + 1], None, ALU.add)
                    a.then_inc(TV.sem, 1)
                    dve.wait_ge(TV.sem, TV.at(f, "o_add"))
                    stats(TV, f, ("o_stats", "o_aggr"), o, tstat, tmv)
                    dve.tensor_scalar(tsm[:, 0, :], tmv[:, :, 1], LN_EPS, None, ALU.add).then_inc(TV.sem, 1)
                    dve.wait_ge(TV.sem, TV.at(f, "o_w"))
                if n == 2:
                    dve.wait_ge(TA.sem, TA.at(f, "o_ex"))
                    newton(TV, f, ("o_n1", "o_n2", "o_n3", "o_r"), tsm, 0, tsm[:, 3, :])
                    minus_mean(TV, f, "o_nmr", tsm[:, 4, :], tmv, tsm[:, 3, :], False)
                if n == 3:
                    dve.wait_ge(TA.sem, TA.at(f, "o_norm"))
                    dve.tensor_tensor(x1[:, :, :], xt[:, :, :], o[:, :, :], ALU.add).then_inc(TV.sem, 1)
                    dve.wait_ge(TV.sem, TV.at(f, "x1"))
                    stats(TV, f, ("x_stats", "x_aggr"), x1, tstat, tmv)
                    dve.tensor_scalar(tsm[:, 5, :], tmv[:, :, 1], LN_EPS, None, ALU.add).then_inc(TV.sem, 1)
                    dve.wait_ge(TV.sem, TV.at(f, "x_w"))
                if n == 4:
                    dve.wait_ge(TA.sem, TA.at(f, "x_ex"))
                    newton(TV, f, ("x_n1", "x_n2", "x_n3", "x_r"), tsm, 5, tsm[:, 8, :])
                    minus_mean(TV, f, "x_nmr", tsm[:, 9, :], tmv, tsm[:, 8, :], False)
                if n in (6, 7):
                    for m in range(4 * (n - 6), 4 * (n - 5)):
                        dve.wait_ge(TA.sem, TA.at(f, f"a{m}"))
                        dve.tensor_scalar(G[:, m, :], bank(2 + m)[:, 1, :], c_("w2_s", m), None,
                                          ALU.mult).then_inc(TV.sem, 1)
                if n == 15:
                    dve.wait_ge(TP.sem, TP.at(f, "w3"))
                    dve.tensor_tensor(fo[:, :, :], bank(18)[:, :, :], s_3[:, None, :].broadcast_to([P, TT, DM]), ALU.mult).then_inc(TV.sem, 1)
                    dve.wait_ge(TV.sem, TV.at(f, "f_out"))
                    stats(TV, f, ("f_stats", "f_aggr"), fo, tstat, tmv)
                    dve.tensor_scalar(tsm[:, 10, :], tmv[:, :, 1], LN_EPS, None, ALU.add).then_inc(TV.sem, 1)
                    dve.wait_ge(TV.sem, TV.at(f, "f_w"))
                    dve.wait_ge(TA.sem, TA.at(f, "f_ex"))
                    newton(TV, f, ("f_n1", "f_n2", "f_n3", "f_r"), tsm, 10, tsm[:, 13, :])
                    minus_mean(TV, f, "f_nmr", tsm[:, 14, :], tmv, tsm[:, 13, :], False)
                    dve.wait_ge(TA.sem, TA.at(f, "f_norm"))
                    dve.wait_ge(out_stored.sem, out_stored.at(f - 1, "landed"))
                    dve.tensor_tensor(ob[:, :, :], x1[:, :, :], fo[:, :, :], ALU.add).then_inc(TV.sem, 1)

            def body(c, par, scan=False, head=False, tail=False, j=None):
                at_start = None if j is None else (j * 2 == CHUNKS_PER_SEQ - 2)
                if scan and j is not None and par == 0:
                    with dve.If(at_start):
                        dve.memset(carry[:, :, :], 0.0).then_inc(carry_clear, 1)
                    with dve.Else():
                        dve.engine_nop().then_inc(carry_clear, 1)
                    dve.wait_ge(carry_clear, j + 2)
                for n in range(SLOTS):
                    if scan:
                        back(c, par, n)
                    if tail:
                        tail_step(c - 1, 1 - par, n)
                    if head:
                        first = True if j is None and par == 1 else (at_start if j is not None and par == 1 else None)
                        head_step(c + 1, 1 - par, n, j, first)

            iterate(body, dve)


def kernel(**inputs):
    import numpy as _np
    import concourse.bacc as _bacc
    from concourse import mybir as _mybir
    from concourse.bass_utils import run_bass_kernel_spmd as _run

    p = 128
    a = {k: _np.asarray(v) for k, v in inputs.items()}
    A, F = "L0_attn_", "L0_ffn_"

    def tiles(v):
        return v.reshape(v.shape[0] // p, p, -1).transpose(1, 0, 2).reshape(p, -1)

    arrays = {
        "x": a[A + "x"],
        "in_proj": a[A + "in_proj_w"].T, "x_proj": a[A + "x_proj_w"].T,
        "dt_proj": a[A + "dt_proj_w"].T, "out_proj": a[A + "out_proj_w"].T,
        "w1": a[F + "w1_w"].T, "w2": a[F + "w2_w"].T,
        "h1": a[F + "h1_w"].T, "h2": a[F + "h2_w"].T, "w3": a[F + "w3_w"].T,
        "cols": _np.concatenate([tiles(a[k]) for k in (
            A + "conv_w", A + "conv_b", A + "dt_proj_b", A + "D", A + "A_log", A + "norm_w",
            F + "w1_s", F + "w2_s", F + "h1_s", F + "h2_s")], axis=1),
        "w3_s": a[F + "w3_s"],
    }
    arrays = {f"in_{k}": _np.ascontiguousarray(v) for k, v in arrays.items()}
    nc = _bacc.Bacc("TRN2", target_bir_lowering=False, num_devices=1)
    args = [nc.dram_tensor(k, v.shape, _mybir.dt.from_np(v.dtype), kind="ExternalInput").ap()
            for k, v in arrays.items()]
    args.append(nc.dram_tensor("out_0", a[A + "x"].shape, _mybir.dt.float32, kind="ExternalOutput").ap())
    build(nc, *args)
    r = _run(nc, [arrays], core_ids=[0])
    return r.results[0]["out_0"]
```

```python
from contextlib import ExitStack

import concourse.bass as bass
from concourse import mybir

ALU = mybir.AluOpType
ACT = mybir.ActivationFunctionType
AX = mybir.AxisListType
F32 = mybir.dt.float32
F32R = mybir.dt.float32r
I32 = mybir.dt.int32

P = 128
T = 256
TT = T // P
LN_EPS = 1e-5
RMS_EPS = 1.1920928955078125e-07
LN_EXP = "natural_log_exp_and_others"


class Steps:

    def __init__(self, sem, names):
        self.sem, self.names = sem, list(names)
        self.per_chunk = len(self.names)

    def at(self, chunk, name):
        return chunk * self.per_chunk + (2 * self.per_chunk + self.names.index(name) + 1)

    def piece(self, chunk, index):
        return chunk * (16 * self.per_chunk) + index * 16 + (2 * self.per_chunk + 1) * 16


def build(nc, x, in_proj, x_proj, dt_proj, out_proj, w1, w2, h1, h2, w3, cols, w3_s, out):
    B, L, DM = x.shape
    R, DI = dt_proj.shape
    N = (x_proj.shape[1] - R) // 2
    HID = w1.shape[1]
    CONV = 4
    DT, KM, HM = DI // P, DM // P, HID // P
    CHUNKS = B * L // T
    PER_SEQ = L // T
    assert B == 2 and PER_SEQ % 2 == 0 and N % 2 == 0 and (DT, KM, HM, TT) == (4, 2, 8, 2) and DM == T

    at, col_at = 0, {}
    for name, width in (("conv_w", DT * CONV), ("conv_b", DT), ("dt_b", DT), ("D", DT), ("A_log", DT * N),
                        ("norm_w", KM), ("w1_s", HM), ("w2_s", HM), ("h1_s", HM), ("h2_s", HM)):
        col_at[name] = at
        at += width
    COLS = at

    x_in = x.rearrange("b (c t p) d -> (b c) p t d", t=TT, p=P)
    x_out = out.rearrange("b (c t p) d -> (b c) p t d", t=TT, p=P)

    ctx = ExitStack()
    with ctx:
        def sb(name, shape, dt=F32):
            return ctx.enter_context(nc.sbuf_tensor(name, shape, dt))

        def pb(name, shape):
            return ctx.enter_context(nc.psum_tensor(name, shape, F32))

        def sem(name):
            return ctx.enter_context(nc.semaphore(name))

        w_in = sb("w_in", [P, KM, 2 * DI])
        w_bc = sb("w_bc", [P, DT, 2, 2 * N])
        w_dtx = sb("w_dtx", [P, DT, R])
        w_dt = sb("w_dt", [R, DI])
        w_out = sb("w_out", [P, DT, DM])
        w_1 = sb("w_1", [P, KM, HID], F32R)
        w_2 = sb("w_2", [P, KM, HID], F32R)
        w_h1 = sb("w_h1", [P, HM, HID], F32R)
        w_h2 = sb("w_h2", [P, HM, HID], F32R)
        w_3 = sb("w_3", [P, HM, DM], F32R)
        s_3 = sb("s_3", [P, DM])
        col = sb("col", [P, COLS])
        A = sb("A", [P, DT * N])
        ident = sb("ident", [P, P])
        ones = sb("ones", [P, 1])
        pick = sb("pick", [4 * N, 2 * N], F32R)

        xh = sb("xh", [P, TT, DM])
        u_ext = sb("u_ext", [P, DT, CONV - 1 + T])
        uc = [sb(f"uc{i}", [P, DT, T]) for i in range(2)]
        z = [sb(f"z{i}", [P, DT, T]) for i in range(2)]
        delta = [sb(f"delta{i}", [P, DT, T]) for i in range(2)]
        X = [sb(f"X{i}", [P, DT, T]) for i in range(2)]
        BC = [sb(f"BC{i}", [4 * N, T], F32R) for i in range(2)]
        e_sp = sb("e_sp", [P, DT, T])
        hn = e_sp[:, 0:2, :]
        hT = e_sp[:, 2:4, :]
        dtx = e_sp[0:R, 3, :]
        hstat = sb("hstat", [P, TT, 6])
        hmv = sb("hmv", [P, TT, 2])
        hsm = sb("hsm", [P, 14, TT])

        dA = [sb(f"dA{i}", [P, DT, T]) for i in range(2)]
        Bs = [sb(f"Bs{i}", [P, T]) for i in range(2)]
        S = [sb(f"S{i}", [P, DT, T]) for i in range(3)]
        gate = sb("gate", [P, 1])
        carry = sb("carry", [P, N, DT])

        xt = sb("xt", [P, TT, DM])
        o = sb("o", [P, TT, DM])
        x1 = [sb(f"x1{i}", [P, TT, DM]) for i in range(2)]
        fo = sb("fo", [P, TT, DM])
        Rw = sb("Rw", [P, HM, T])
        Ghi = sb("Ghi", [P, HM, T], F32R)
        Glo = sb("Glo", [P, HM, T], F32R)
        xfT_hi, xfT_lo = Ghi[:, 0:KM, :], Glo[:, 0:KM, :]
        mr = [sb(f"mr{i}", [P, 2, TT]) for i in range(2)]
        mr_tail = sb("mr_tail", [P, 2, TT])
        tstat = sb("tstat", [P, TT, 6])
        tmv = sb("tmv", [P, TT, 2])
        tsm = sb("tsm", [P, 10, TT])
        fstat = sb("fstat", [P, TT, 6])
        fmv = sb("fmv", [P, TT, 2])
        fsm = sb("fsm", [P, 5, TT])

        SC = HID
        w_lo = sb("w_lo", [P, 2 * P], F32R)
        STAGES = [(w, src, k) for w, src, n in ((w_1, w1, KM), (w_2, w2, KM), (w_h1, h1, HM), (w_h2, h2, HM))
                  for k in range(n)] + [(w_3, w3, k) for k in range(0, HM, SC // DM)]
        lo_sum = sb("lo_sum", [P, len(STAGES)])
        lo_all = sb("lo_all", [P, 1])
        inexact = sb("inexact", [1, 1], I32)
        LAYER_PIECES = HM * HM // 2
        TAIL_PIECES = 2 * HM + LAYER_PIECES
        lo_tail = nc.dram_tensor("lo_tail", (TAIL_PIECES, P, 2 * P), F32, kind="Internal").ap()
        END_PIECES = LAYER_PIECES + TT * HM
        lo_end = nc.dram_tensor("lo_end", (LAYER_PIECES + HM, P, 2 * P), F32, kind="Internal").ap()

        yP = pb("yP", [P, DT, T])
        bP = [pb(f"bP{i}", [P, 2, T]) for i in range(2)]
        hP = [pb(f"hP{i}", [P, 2, T]) for i in range(2)]
        fP = [pb(f"fP{i}", [P, 2, T]) for i in range(2)]

        def c_(name, i, n=1):
            return col[:, col_at[name] + i:col_at[name] + i + n]

        head_vec = Steps(sem("head_vec"),
                         ["x_stats", "x_aggr", "w", "n1", "n2", "n3", "r1", "q1", "q2", "w2", "nmr1",
                          "m1", "m2", "m3", "r2", "r12", "nmr12", "halo", "tap0", "tap1", "tap2",
                          "bc_hi", "bc_lo", "t1"])
        scan_vec = Steps(sem("scan_vec"),
                         [f"{k}{n}" for n in range(N) for k in ("s0_", "s1_", "s2_", "s3_", "carry", "g")])
        tail_vec = Steps(sem("tail_vec"),
                         ["mr", "y_d", "yz", "o_mul", "o_add", "o_stats", "o_aggr", "o_w", "o_n1", "o_n2", "o_n3",
                          "o_r", "o_nmr", "x1", "x_stats", "x_aggr", "x_w", "x_n1", "x_n2", "x_n3", "x_r",
                          "x_nmr", "xf_lo"] + [f"b{m}" for m in range(HM)])
        end_vec = Steps(sem("end_vec"),
                        ["out", "stats", "aggr", "w", "n1", "n2", "n3", "r", "nmr", "sum"])
        head_act = Steps(sem("head_act"),
                         ["ln1", "ex1", "ln2", "ex2", "hn", "hT", "u0", "u1", "cbase", "silu_u", "z0", "z1",
                          "dtx", "v0", "v1", "e", "l"])
        scan_act = Steps(sem("scan_act"),
                         [f"{k}{n}" for n in range(N) for k in ("b", "e0_", "e1_", "e2_", "e3_")])
        tail_act = Steps(sem("tail_act"),
                         ["o_ln", "o_ex", "o_norm", "x_ln", "x_ex", "xf", "xf_hi"] + [f"a{m}" for m in range(HM)]
                         + ["silu", "hi0_0", "hi0_1"] + [f"h1_{m}" for m in range(HM)])
        end_act = Steps(sem("end_act"), ["gelu1", "hi1_0", "hi1_1"] + [f"h2_{m}" for m in range(HM)]
                        + ["gelu2", "hi2_0", "hi2_1", "ln", "ex", "norm"])
        head_pe = Steps(sem("head_pe"), ["hT", "u0", "u1", "z0", "z1", "xp", "d0", "d1"])
        bcast_pe = Steps(sem("bcast_pe"), [f"b{n}" for n in range(N)])
        sum_pe = Steps(sem("sum_pe"), [f"y{n}" for n in range(N)])
        tail_pe = Steps(sem("tail_pe"),
                        ["out", "xfT"] + [f"ab{m}" for m in range(HM)] + [f"h1_{m}" for m in range(HM)])
        end_pe = Steps(sem("end_pe"), [f"h2_{m}" for m in range(HM)] + ["w3"])
        head_pool = Steps(sem("head_pool"), ["res", "log1p", "delta", "X"])
        scan_pool = Steps(sem("scan_pool"), [f"dBu{n}" for n in range(N)])
        tail_pool = Steps(sem("tail_pool"), ["gated0", "gated1", "lo0_0", "lo0_1"])
        end_pool = Steps(sem("end_pool"), ["lo1_0", "lo1_1", "lo2_0", "lo2_1"])
        xh_in = Steps(sem("xh_in"), ["dma"] * 15 + ["landed"])
        xt_in = Steps(sem("xt_in"), ["dma"] * 15 + ["landed"])
        out_stored = Steps(sem("out_stored"), ["dma"] * 15 + ["landed"])
        tail_lo_in = Steps(sem("tail_lo_in"), range(TAIL_PIECES))
        tail_lo_used = Steps(sem("tail_lo_used"), range(TAIL_PIECES))
        end_lo_in = Steps(sem("end_lo_in"), range(END_PIECES))
        end_lo_used = Steps(sem("end_lo_used"), range(END_PIECES))

        small_in = sem("small_in")
        stage_in = [sem(f"stage_in{i}") for i in range(3)]
        stage_hi = sem("stage_hi")
        stage_lo = sem("stage_lo")
        stage_abs = sem("stage_abs")
        lo_stored = [sem(f"lo_stored{i}") for i in range(2)]
        lo_added = sem("lo_added")
        lo_total = sem("lo_total")
        ident_made = sem("ident_made")
        pick_made = sem("pick_made")
        A_made = sem("A_made")
        carry_clear = sem("carry_clear")

        SMALL = 8
        S_flat = [s[:, :, :].rearrange("p a b -> p (a b)") for s in S]
        dA_flat = [s[:, :, :].rearrange("p a b -> p (a b)") for s in dA]

        def start(eng, *steps):
            for s in steps:
                eng.sem_inc(s.sem, 2 * s.per_chunk)

        def iterate(engine, body):
            body(-1, 1, head=True, prepare=True)
            body(0, 0, scan=True, head=True)
            body(1, 1, scan=True, head=True, tail=True)
            with engine.Fori(0, CHUNKS // 2 - 2) as j:
                body(j * 2 + 2, 0, scan=True, head=True, tail=True, end=True,
                     seq_start=(j * 2 == PER_SEQ - 2), j=j)
                body(j * 2 + 3, 1, scan=True, head=True, tail=True, end=True,
                     head_seq_start=(j * 2 == PER_SEQ - 4))
            body(CHUNKS - 2, 0, scan=True, head=True, tail=True, end=True)
            body(CHUNKS - 1, 1, scan=True, tail=True, end=True)
            body(CHUNKS, 0, tail=True, end=True)
            body(CHUNKS + 1, 1, end=True)

        HALVES = 2 * N

        def slot(par, n):
            return (n + par) % 3

        def slot_before(c, par, n):
            for m in range(n - 1, -1, -1):
                if slot(par, m) == slot(par, n):
                    return c, f"y{m}"
            for m in range(N - 1, -1, -1):
                if slot(1 - par, m) == slot(par, n):
                    return c - 1, f"y{m}"

        USES = (["h2_0", "h2_1", "out"] + [f"h2_{m}" for m in range(2, HM)] + ["xfT", "w3"]
                + [f"ab{m}" for m in range(HM)] + [f"h1_{m}" for m in range(HM)])

        def ring(par, use):
            return fP[(par + USES.index(use)) % 2]

        def last_reader(c, use, tail=True, end=True):
            def reader(c, name):
                if name == "out":
                    return tail_vec, c - 1, "o_mul"
                if name == "xfT":
                    return tail_vec, c - 1, "xf_lo"
                if name == "w3":
                    return end_vec, c - 2, "out"
                if name.startswith("h2"):
                    return end_act, c - 2, name
                if name.startswith("h1"):
                    return tail_act, c - 1, name
                return tail_vec, c - 1, name.replace("ab", "b")
            assert len(USES) % 2 == 1
            at = USES.index(use) - 2
            while at >= 0:
                of_end = USES[at] == "w3" or USES[at].startswith("h2")
                if end if of_end else tail:
                    return reader(c, USES[at])
                at -= 2
            return reader(c - 1, USES[at + len(USES)])

        block = ctx.enter_context(nc.Block())

        @block.sync
        def _(sp):
            start(sp, xh_in, xt_in, out_stored, tail_lo_in, end_lo_in)
            sp.sem_inc(tail_lo_in.sem, 30 * TAIL_PIECES)
            sp.sem_inc(end_lo_in.sem, 30 * END_PIECES)
            sp.dma_start(xh[:, :, :], x_in[0]).then_inc(xh_in.sem, 16)
            sp.dma_start(col[:, :], cols).then_inc(small_in, 16)
            sp.dma_start(w_in[:, :, :], in_proj.rearrange("(k p) n -> p k n", p=P)).then_inc(small_in, 16)
            xp = x_proj.rearrange("(k p) n -> p k n", p=P)
            sp.dma_start(w_dtx[:, :, :], xp[:, :, 0:R]).then_inc(small_in, 16)
            sp.dma_start(w_bc[:, :, 0, :], xp[:, :, R:R + 2 * N]).then_inc(small_in, 16)
            sp.dma_start(w_bc[:, :, 1, :], xp[:, :, R:R + 2 * N]).then_inc(small_in, 16)
            sp.dma_start(w_dt[:, :], dt_proj).then_inc(small_in, 16)
            sp.dma_start(w_out[:, :, :], out_proj.rearrange("(k p) n -> p k n", p=P)).then_inc(small_in, 16)
            sp.dma_start(s_3[:, :], w3_s.partition_broadcast(P)).then_inc(small_in, 16)
            for s, (w, src, k) in enumerate(STAGES):
                if s >= 3:
                    sp.wait_ge(stage_abs, s - 2)
                rows = src.rearrange("(k p) n -> p k n", p=P)
                n = SC // src.shape[1]
                sp.dma_start(S_flat[s % 3].rearrange("p (k n) -> p k n", k=n), rows[:, k:k + n, :])\
                  .then_inc(stage_in[s % 3], 16)
            sp.wait_ge(lo_added, 2)
            some_lo = sp.value_load(inexact[0:1, 0:1], min_val=0, max_val=1)

            def body(c, par, scan=False, head=False, tail=False, end=False, prepare=False,
                     seq_start=None, head_seq_start=None, j=None):
                if end:
                    with sp.If(some_lo != 0):
                        for first, n, skip in ((0, LAYER_PIECES + HM, 0), (LAYER_PIECES, HM, HM)):
                            with sp.Fori(first, first + n) as k:
                                sp.wait_ge(tail_lo_used.sem, tail_lo_used.at(c - 2, TAIL_PIECES - 1))
                                sp.wait_ge(end_lo_used.sem, end_lo_used.at(c - 2, 0) - 1 + skip + k)
                                sp.dma_start(w_lo[:, :].bitcast(F32), lo_end[k]).then_inc(end_lo_in.sem, 16)
                    with sp.Else():
                        sp.nop()
                    sp.wait_ge(end_vec.sem, end_vec.at(c - 2, "sum"))
                    sp.dma_start(x_out[c - 2], x1[par][:, :, :]).then_inc(out_stored.sem, 16)
                if head and not (isinstance(c, int) and c + 2 >= CHUNKS):
                    sp.wait_ge(head_act.sem, head_act.at(c + 1, "hn"))
                    sp.dma_start(xh[:, :, :], x_in[c + 2]).then_inc(xh_in.sem, 16)
                if scan:
                    sp.wait_ge(tail_vec.sem, tail_vec.at(c - 1, "x1"))
                    sp.dma_start(xt[:, :, :], x_in[c]).then_inc(xt_in.sem, 16)
                if tail:
                    with sp.If(some_lo != 0):
                        with sp.Fori(0, TAIL_PIECES) as k:
                            sp.wait_ge(end_lo_used.sem, end_lo_used.at(c - 2, END_PIECES - 1))
                            sp.wait_ge(tail_lo_used.sem, tail_lo_used.at(c - 1, 0) - 1 + k)
                            sp.dma_start(w_lo[:, :].bitcast(F32), lo_tail[k]).then_inc(tail_lo_in.sem, 16)
                    with sp.Else():
                        sp.nop()

            iterate(sp, body)
            sp.wait_ge(out_stored.sem, out_stored.at(CHUNKS - 1, "landed"))

        @block.gpsimd
        def _(pool):
            start(pool, head_pool, scan_pool, tail_pool, end_pool)
            pool.memset(ones[:, :], 1.0).then_inc(ident_made, 1)
            pool.memset(ident[:, :], 0.0).then_inc(ident_made, 1)
            pool.wait_ge(ident_made, 2)
            pool.affine_select(out=ident[:, :], in_=ident[:, :], compare_op=ALU.not_equal, fill=1.0,
                               base=0, pattern=[[-1, P]], channel_multiplier=1).then_inc(ident_made, 1)

            def store_lo(s):
                w, src, k = STAGES[s]
                pool.wait_ge(stage_lo, s + 1)
                lo = dA_flat[s % 2].rearrange("p (m c) -> p m c", c=P)
                if w is w_3:
                    dst = lo_end[LAYER_PIECES + k:LAYER_PIECES + k + SC // DM].rearrange("k p n -> p k n")
                    lo = dA_flat[s % 2].rearrange("p (k n) -> p k n", n=DM)
                elif w is w_1 or w is w_2:
                    i = 0 if w is w_1 else 1
                    dst = lo_tail[0:2 * HM].rearrange("(m i) p (k c) -> k i p m c", i=2, k=2)[k, i]
                else:
                    layer = lo_tail[2 * HM:TAIL_PIECES] if w is w_h1 else lo_end[0:LAYER_PIECES]
                    dst = layer.rearrange("(m q) p (k c) -> q k p m c", m=HM, k=2)[k // 2, k % 2]
                pool.dma_start(dst, lo).then_inc(lo_stored[s % 2], 16)

            def front(c, par, n):
                pool.wait_ge(scan_act.sem, scan_act.at(c, f"b{n}"))
                if n == 0:
                    pool.wait_ge(head_pool.sem, head_pool.at(c, "X"))
                before, read = slot_before(c, par, n)
                pool.wait_ge(sum_pe.sem, sum_pe.at(before, read))
                pool.tensor_tensor(S[slot(par, n)][:, :, :], X[par][:, :, :],
                                   Bs[n % 2][:, None, :].broadcast_to([P, DT, T]),
                                   ALU.mult).then_inc(scan_pool.sem, 1)

            def head_step(h, hp, hs):
                if hs == 26:
                    pool.wait_ge(head_vec.sem, head_vec.at(h, "t1"))
                    pool.tensor_tensor(X[hp][:, :, :], e_sp[:, :, :], X[hp][:, :, :],
                                       ALU.subtract).then_inc(head_pool.sem, 1)
                if hs == 27:
                    pool.wait_ge(head_pool.sem, head_pool.at(h, "res"))
                    pool.wait_ge(head_act.sem, head_act.at(h, "l"))
                    pool.tensor_tensor(X[hp][:, :, :], X[hp][:, :, :], e_sp[:, :, :],
                                       ALU.add).then_inc(head_pool.sem, 1)
                if hs == 28:
                    pool.wait_ge(head_pool.sem, head_pool.at(h, "log1p"))
                    pool.tensor_tensor(delta[hp][:, :, :], delta[hp][:, :, :], X[hp][:, :, :],
                                       ALU.add).then_inc(head_pool.sem, 1)
                if hs == 29:
                    pool.wait_ge(head_pool.sem, head_pool.at(h, "delta"))
                    pool.tensor_tensor(X[hp][:, :, :], delta[hp][:, :, :], uc[hp][:, :, :],
                                       ALU.mult).then_inc(head_pool.sem, 1)

            def tail_step(f, fp, hs):
                if hs in (20, 21):
                    i = hs - 20
                    half = slice(i * HM // 2, (i + 1) * HM // 2)
                    if i == 0:
                        pool.wait_ge(tail_act.sem, tail_act.at(f, "silu"))
                    pool.wait_ge(tail_vec.sem, tail_vec.at(f, f"b{HM // 2 * (i + 1) - 1}"))
                    other = (X[fp], e_sp)[i]
                    pool.tensor_tensor(Rw[:, half, :], Rw[:, half, :], other[:, :, :],
                                       ALU.mult).then_inc(tail_pool.sem, 1)
                if hs in (22, 23):
                    i = hs - 22
                    half = slice(i * HM // 2, (i + 1) * HM // 2)
                    pool.wait_ge(tail_act.sem, tail_act.at(f, f"hi0_{i}"))
                    pool.tensor_tensor(Glo[:, half, :], Rw[:, half, :], Ghi[:, half, :].bitcast(F32),
                                       ALU.subtract).then_inc(tail_pool.sem, 1)

            def end_step(g, gp, hs):
                if hs in (0, 1, 11, 12):
                    layer, i = (1, hs) if hs < 2 else (2, hs - 11)
                    half = slice(i * HM // 2, (i + 1) * HM // 2)
                    pool.wait_ge(end_act.sem, end_act.at(g, f"hi{layer}_{i}"))
                    pool.tensor_tensor(Glo[:, half, :], Rw[:, half, :], Ghi[:, half, :].bitcast(F32),
                                       ALU.subtract).then_inc(end_pool.sem, 1)

            def body(c, par, scan=False, head=False, tail=False, end=False, prepare=False,
                     seq_start=None, head_seq_start=None, j=None):
                for hs in range(HALVES):
                    n = hs // 2
                    if prepare and hs < len(STAGES):
                        store_lo(hs)
                    if scan and hs % 2 == 0 and n + 1 < N:
                        front(c, par, n + 1)
                    if head and hs == HALVES - 2:
                        front(c + 1, 1 - par, 0)
                    if end:
                        end_step(c - 2, par, hs)
                    if tail:
                        tail_step(c - 1, 1 - par, hs)
                    if head:
                        head_step(c + 1, 1 - par, hs)

            iterate(pool, body)
            for i in range(2):
                pool.wait_ge(lo_stored[i], 16 * len(STAGES[i::2]))

        @block.tensor
        def _(pe):
            start(pe, head_pe, bcast_pe, sum_pe, tail_pe, end_pe, tail_lo_used, end_lo_used)
            pe.wait_ge(ident_made, 3)
            pe.wait_ge(small_in, 16 * SMALL)
            pe.wait_ge(pick_made, 1)
            some_lo = [None]

            def products(dst, lhs, rhs, k):
                for i in range(k):
                    mm = pe.matmul(dst, lhs(i), rhs(i), start=(i == 0), stop=(i == k - 1))
                return mm

            def split_products(dst, w, cols_, hi, lo, k, used, landed, chunk, piece):
                for i in range(k):
                    pe.matmul(dst, w[:, i, cols_], hi[:, i, :], start=(i == 0), stop=False)
                    if piece is not None:
                        if i % 2 == 0:
                            pe.wait_ge(landed.sem, landed.piece(chunk, piece + i // 2))
                        part = w_lo[:, (i % 2) * P:(i % 2 + 1) * P]
                        pe.matmul(dst, part, hi[:, i, :], start=False, stop=False)
                        mm = pe.matmul(dst, part, lo[:, i, :], start=False, stop=False)
                        if i % 2 == 1:
                            mm.then_inc(used.sem, 1)
                    mm = pe.matmul(dst, w[:, i, cols_], lo[:, i, :], start=False, stop=(i == k - 1))
                return mm

            def bcast(c, par, n):
                if n == 0:
                    pe.wait_ge(head_vec.sem, head_vec.at(c, "bc_lo"))
                if n >= 2:
                    pe.wait_ge(scan_vec.sem, scan_vec.at(c, f"g{n - 2}"))
                else:
                    pe.wait_ge(scan_vec.sem, scan_vec.at(c - 1, f"g{N - 2 + n}"))
                for i, r in ((0, n), (1, N + n)):
                    mm = pe.matmul(bP[n % 2][:, i, :], pick[:, r:r + 1].broadcast_to([4 * N, P]), BC[par][:, :],
                                   start=True, stop=True)
                mm.then_inc(bcast_pe.sem, 1)

            def state_sum(c, par, n):
                pe.wait_ge(scan_vec.sem, scan_vec.at(c, f"g{n}"))
                if n == 0:
                    pe.wait_ge(tail_vec.sem, tail_vec.at(c - 1, "y_d"))
                for i in range(DT // 2):
                    mm = pe.matmul(yP[:, 2 * i:2 * i + 2, :], ident[:, :], S[slot(par, n)][:, 2 * i:2 * i + 2, :],
                                   start=(n == 0), stop=(n == N - 1))
                mm.then_inc(sum_pe.sem, 1)

            def head_step(h, hp, hs):
                if hs == 5:
                    pe.wait_ge(head_act.sem, head_act.at(h, "hn"))
                    pe.wait_ge(head_act.sem, head_act.at(h - 1, "v0"))
                    for k in range(KM):
                        for t in range(TT):
                            mm = pe.transpose(hP[0][:, k, t * P:(t + 1) * P], hn[:, t, k * P:(k + 1) * P],
                                              ident[:, :])
                    mm.then_inc(head_pe.sem, 1)
                if hs in (7, 8, 10, 11):
                    for q in ((7, 8, 10, 11).index(hs),):
                        if q == 0:
                            pe.wait_ge(head_act.sem, head_act.at(h, "hT"))
                            pe.wait_ge(head_act.sem, head_act.at(h - 1, "v1"))
                        else:
                            pe.wait_ge(head_act.sem, head_act.at(h, ("hT", "u0", "u1")[q - 1]))
                        for d in range(2):
                            m = 2 * q + d
                            mm = products(hP[(q + 1) % 2][:, d, :], lambda k: w_in[:, k, m * P:(m + 1) * P],
                                          lambda k: hT[:, k, :], KM)
                        mm.then_inc(head_pe.sem, 1)
                if hs == 20:
                    pe.wait_ge(head_act.sem, head_act.at(h, "z0"))
                    products(hP[1][0:4 * N, 0, :], lambda k: w_bc[:, k, :, :].rearrange("p a n -> p (a n)"),
                             lambda k: uc[hp][:, k, :], DT)
                if hs == 21:
                    products(hP[1][0:R, 1, :], lambda k: w_dtx[:, k, :],
                             lambda k: uc[hp][:, k, :], DT).then_inc(head_pe.sem, 1)
                if hs == 23:
                    pe.wait_ge(head_act.sem, head_act.at(h, "dtx"))
                    for q in range(2):
                        if q == 1:
                            pe.wait_ge(head_vec.sem, head_vec.at(h, "bc_lo"))
                        for d in range(2):
                            m = 2 * q + d
                            mm = pe.matmul(hP[q][:, d, :], w_dt[:, m * P:(m + 1) * P], dtx, start=True, stop=True)
                        mm.then_inc(head_pe.sem, 1)

            def branches(f, fp, m, lo):
                if m == 0:
                    pe.wait_ge(tail_vec.sem, tail_vec.at(f, "xf_lo"))
                steps, chunk, name = last_reader(f + 1, f"ab{m}")
                pe.wait_ge(steps.sem, steps.at(chunk, name))
                for i, w in enumerate((w_1, w_2)):
                    mm = split_products(ring(1 - fp, f"ab{m}")[:, i, :], w, slice(m * P, (m + 1) * P),
                                        xfT_hi, xfT_lo, KM, tail_lo_used, tail_lo_in, f, 2 * m + i if lo else None)
                mm.then_inc(tail_pe.sem, 1)

            def hidden1(f, fp, m, lo):
                if m == 0:
                    pe.wait_ge(tail_pool.sem, tail_pool.at(f, "lo0_1"))
                steps, chunk, name = last_reader(f + 1, f"h1_{m}")
                pe.wait_ge(steps.sem, steps.at(chunk, name))
                piece = 2 * HM + m * (HM // 2)
                split_products(ring(1 - fp, f"h1_{m}")[:, 0, :], w_h1, slice(m * P, (m + 1) * P), Ghi, Glo, HM,
                               tail_lo_used, tail_lo_in, f, piece if lo else None).then_inc(tail_pe.sem, 1)

            def hidden2(g, gp, m, lo, tail):
                if m == 0:
                    pe.wait_ge(end_pool.sem, end_pool.at(g, "lo1_1"))
                steps, chunk, name = last_reader(g + 2, f"h2_{m}", tail=tail)
                pe.wait_ge(steps.sem, steps.at(chunk, name))
                split_products(ring(gp, f"h2_{m}")[:, 0, :], w_h2, slice(m * P, (m + 1) * P), Ghi, Glo, HM,
                               end_lo_used, end_lo_in, g, m * (HM // 2) if lo else None).then_inc(end_pe.sem, 1)

            def last_product(g, gp, lo, tail):
                pe.wait_ge(end_pool.sem, end_pool.at(g, "lo2_1"))
                steps, chunk, name = last_reader(g + 2, "w3", tail=tail)
                pe.wait_ge(steps.sem, steps.at(chunk, name))
                for t in range(TT):
                    dst = ring(gp, "w3")[:, t, :]
                    tok = slice(t * P, (t + 1) * P)
                    for k in range(HM):
                        pe.matmul(dst, Ghi[:, k, tok], w_3[:, k, :], start=(k == 0), stop=False)
                        if lo:
                            pe.wait_ge(end_lo_in.sem, end_lo_in.piece(g, LAYER_PIECES + t * HM + k))
                            pe.matmul(dst, Ghi[:, k, tok], w_lo[:, :], start=False, stop=False)
                            pe.matmul(dst, Glo[:, k, tok], w_lo[:, :], start=False,
                                      stop=False).then_inc(end_lo_used.sem, 1)
                        mm = pe.matmul(dst, Glo[:, k, tok], w_3[:, k, :], start=False, stop=(k == HM - 1))
                mm.then_inc(end_pe.sem, 1)

            def tail_step(f, fp, hs):
                if hs == 3:
                    pe.wait_ge(tail_vec.sem, tail_vec.at(f, "yz"))
                    steps, chunk, name = last_reader(f + 1, "out")
                    pe.wait_ge(steps.sem, steps.at(chunk, name))
                    for t in range(TT):
                        mm = products(ring(1 - fp, "out")[:, t, :], lambda k: z[fp][:, k, t * P:(t + 1) * P],
                                      lambda k: w_out[:, k, :], DT)
                    mm.then_inc(tail_pe.sem, 1)
                if hs == 12:
                    pe.wait_ge(tail_act.sem, tail_act.at(f, "xf"))
                    steps, chunk, name = last_reader(f + 1, "xfT")
                    pe.wait_ge(steps.sem, steps.at(chunk, name))
                    for k in range(KM):
                        for t in range(TT):
                            mm = pe.transpose(ring(1 - fp, "xfT")[:, k, t * P:(t + 1) * P],
                                              o[:, t, k * P:(k + 1) * P], ident[:, :])
                    mm.then_inc(tail_pe.sem, 1)
                if 15 <= hs < 19:
                    with pe.If(some_lo[0] != 0):
                        for m in (2 * hs - 30, 2 * hs - 29):
                            branches(f, fp, m, True)
                    with pe.Else():
                        for m in (2 * hs - 30, 2 * hs - 29):
                            branches(f, fp, m, False)
                if 24 <= hs < 32:
                    with pe.If(some_lo[0] != 0):
                        hidden1(f, fp, hs - 24, True)
                    with pe.Else():
                        hidden1(f, fp, hs - 24, False)

            def end_step(g, gp, hs, tail):
                if 2 <= hs < 10:
                    with pe.If(some_lo[0] != 0):
                        hidden2(g, gp, hs - 2, True, tail)
                    with pe.Else():
                        hidden2(g, gp, hs - 2, False, tail)
                if hs == 13:
                    with pe.If(some_lo[0] != 0):
                        last_product(g, gp, True, tail)
                    with pe.Else():
                        last_product(g, gp, False, tail)

            def body(c, par, scan=False, head=False, tail=False, end=False, prepare=False,
                     seq_start=None, head_seq_start=None, j=None):
                for hs in range(HALVES):
                    n = hs // 2
                    if scan and hs % 2 == 0 and n + 1 < N:
                        bcast(c, par, n + 1)
                    if head and hs == HALVES - 2:
                        bcast(c + 1, 1 - par, 0)
                    if tail and hs == 0:
                        state_sum(c - 1, 1 - par, N - 1)
                    if scan and hs % 2 == 0 and n > 0:
                        state_sum(c, par, n - 1)
                    if end:
                        end_step(c - 2, par, hs, tail)
                    if tail:
                        tail_step(c - 1, 1 - par, hs)
                    if head:
                        head_step(c + 1, 1 - par, hs)
                    if prepare and hs == len(STAGES) + 1:
                        pe.wait_ge(lo_added, 1)
                        pe.matmul(fP[0][0:1, 0, 0:1], lo_all[:, :], ones[:, :], start=True,
                                  stop=True).then_inc(lo_total, 1)
                        pe.wait_ge(lo_added, 2)
                        some_lo[0] = pe.value_load(inexact[0:1, 0:1], min_val=0, max_val=1)

            iterate(pe, body)

        @block.scalar
        def _(act):
            start(act, head_act, scan_act, tail_act, end_act)
            act.wait_ge(small_in, 16 * SMALL)
            act.preload_act_table_set(LN_EXP)
            act.activation(A[:, :], c_("A_log", 0, DT * N), ACT.Exp).then_inc(A_made, 1)
            act.wait_ge(A_made, 1)
            act.mul(A[:, :], A[:, :], -1.0).then_inc(A_made, 1)
            act.wait_ge(A_made, 2)

            def round_stage(s):
                w, src, k = STAGES[s]
                n = SC // src.shape[1]
                act.wait_ge(stage_in[s % 3], 16 * (s // 3 + 1))
                act.copy(w[:, k:k + n, :], S_flat[s % 3].rearrange("p (k n) -> p k n", k=n)).then_inc(stage_hi, 1)

            def sum_stage(s):
                act.wait_ge(stage_lo, s + 1)
                act.activation(S_flat[s % 3], dA_flat[s % 2], ACT.Abs,
                               accum_out=lo_sum[:, s:s + 1]).then_inc(stage_abs, 1)

            def front(c, par, n, first):
                if first:
                    act.wait_ge(bcast_pe.sem, bcast_pe.at(c, f"b{n}"))
                    if n >= 2:
                        act.wait_ge(scan_pool.sem, scan_pool.at(c, f"dBu{n - 2}"))
                    else:
                        act.wait_ge(scan_pool.sem, scan_pool.at(c - 1, f"dBu{N - 2 + n}"))
                    act.copy(Bs[n % 2][:, :], bP[n % 2][:, 0, :]).then_inc(scan_act.sem, 1)
                    if n == 0:
                        act.wait_ge(head_pool.sem, head_pool.at(c, "delta"))
                for d in ((0, 1) if first else (2, 3)):
                    if n >= 2:
                        act.wait_ge(scan_vec.sem, scan_vec.at(c, f"s{d}_{n - 2}"))
                    else:
                        act.wait_ge(scan_vec.sem, scan_vec.at(c - 1, f"s{d}_{N - 2 + n}"))
                    act.activation(dA[n % 2][:, d, :], delta[par][:, d, :], ACT.Exp,
                                   scale=A[:, d * N + n:d * N + n + 1]).then_inc(scan_act.sem, 1)

            def normed(dst, src, sm, r):
                for t in range(TT):
                    a = act.activation(dst[:, t, :], src[:, t, :], ACT.Identity,
                                       scale=sm[:, r, t:t + 1], bias=sm[:, r + 1, t:t + 1])
                return a

            def head_step(h, hp, hs):
                if hs in (1, 2):
                    i, src = hs, (0, 6)[hs - 1]
                    act.wait_ge(head_vec.sem, head_vec.at(h, ("w", "w2")[hs - 1]))
                    act.activation(hsm[:, src + 1, :], hsm[:, src, :], ACT.Ln).then_inc(head_act.sem, 1)
                    act.wait_ge(head_act.sem, head_act.at(h, f"ln{i}"))
                    act.activation(hsm[:, src + 2, :], hsm[:, src + 1, :], ACT.Exp,
                                   scale=-0.5).then_inc(head_act.sem, 1)
                if hs == 4:
                    act.wait_ge(head_vec.sem, head_vec.at(h, "nmr12"))
                    act.wait_ge(head_pool.sem, head_pool.at(h - 1, "log1p"))
                    normed(hn, xh, hsm, 12).then_inc(head_act.sem, 1)
                if hs == 6:
                    act.wait_ge(head_pe.sem, head_pe.at(h, "hT"))
                    for k in range(KM):
                        a = act.activation(hT[:, k, :], hP[0][:, k, :], ACT.Copy, scale=c_("norm_w", k))
                    a.then_inc(head_act.sem, 1)
                if hs == 9:
                    act.wait_ge(head_vec.sem, head_vec.at(h, "halo"))
                    for q in range(2):
                        act.wait_ge(head_pe.sem, head_pe.at(h, f"u{q}"))
                        act.copy(u_ext[:, 2 * q:2 * q + 2, CONV - 1:],
                                 hP[(q + 1) % 2][:, :, :]).then_inc(head_act.sem, 1)
                    act.wait_ge(head_act.sem, head_act.at(h, "u1"))
                    act.wait_ge(tail_pe.sem, tail_pe.at(h - 2, "out"))
                    for d in range(DT):
                        a = act.activation(uc[hp][:, d, :], u_ext[:, d, CONV - 1:], ACT.Identity,
                                           scale=c_("conv_w", d * CONV + CONV - 1), bias=c_("conv_b", d))
                    a.then_inc(head_act.sem, 1)
                if hs == 19:
                    act.wait_ge(head_vec.sem, head_vec.at(h, "tap2"))
                    act.activation(uc[hp][:, :, :], uc[hp][:, :, :], ACT.Silu).then_inc(head_act.sem, 1)
                    for q in range(2):
                        act.wait_ge(head_pe.sem, head_pe.at(h, f"z{q}"))
                        act.activation(z[hp][:, 2 * q:2 * q + 2, :], hP[(q + 1) % 2][:, :, :],
                                       ACT.Silu).then_inc(head_act.sem, 1)
                if hs == 22:
                    act.wait_ge(head_pe.sem, head_pe.at(h, "xp"))
                    act.wait_ge(tail_pool.sem, tail_pool.at(h - 2, "gated1"))
                    act.copy(dtx, hP[1][0:R, 1, :]).then_inc(head_act.sem, 1)
                if hs == 24:
                    act.wait_ge(head_pe.sem, head_pe.at(h, "d1"))
                    for q in range(2):
                        for i in range(2):
                            d = 2 * q + i
                            act.activation(e_sp[:, d, :], hP[q][:, i, :], ACT.Abs, bias=c_("dt_b", d))
                            a = act.activation(delta[hp][:, d, :], hP[q][:, i, :], ACT.Relu, bias=c_("dt_b", d))
                        a.then_inc(head_act.sem, 1)
                    act.wait_ge(head_act.sem, head_act.at(h, "v1"))
                    act.activation(e_sp[:, :, :], e_sp[:, :, :], ACT.Exp, scale=-1.0).then_inc(head_act.sem, 1)
                if hs == 27:
                    act.wait_ge(head_pool.sem, head_pool.at(h, "res"))
                    act.activation(e_sp[:, :, :], e_sp[:, :, :], ACT.Ln, bias=1.0).then_inc(head_act.sem, 1)

            def tail_step(f, fp, hs):
                if hs in (5, 7):
                    s, src = ("o", "x")[hs // 2 - 2], (0, 5)[hs // 2 - 2]
                    act.wait_ge(tail_vec.sem, tail_vec.at(f, f"{s}_w"))
                    act.activation(tsm[:, src + 1, :], tsm[:, src, :], ACT.Ln).then_inc(tail_act.sem, 1)
                    act.wait_ge(tail_act.sem, tail_act.at(f, f"{s}_ln"))
                    act.activation(tsm[:, src + 2, :], tsm[:, src + 1, :], ACT.Exp,
                                   scale=-0.5).then_inc(tail_act.sem, 1)
                if hs == 6:
                    act.wait_ge(tail_vec.sem, tail_vec.at(f, "o_nmr"))
                    normed(o, o, tsm, 3).then_inc(tail_act.sem, 1)
                if hs == 8:
                    act.wait_ge(tail_vec.sem, tail_vec.at(f, "x_nmr"))
                    normed(o, x1[fp], tsm, 8).then_inc(tail_act.sem, 1)
                if hs == 14:
                    act.wait_ge(tail_pe.sem, tail_pe.at(f, "xfT"))
                    act.wait_ge(end_pe.sem, end_pe.at(f - 1, "w3"))
                    act.copy(xfT_hi, ring(1 - fp, "xfT")[:, :, :]).then_inc(tail_act.sem, 1)
                if 15 <= hs < 19:
                    for m in (2 * hs - 30, 2 * hs - 29):
                        act.wait_ge(tail_pe.sem, tail_pe.at(f, f"ab{m}"))
                        act.activation(Rw[:, m, :], ring(1 - fp, f"ab{m}")[:, 0, :], ACT.Copy,
                                       scale=c_("w1_s", m)).then_inc(tail_act.sem, 1)
                if hs == 19:
                    act.wait_ge(tail_act.sem, tail_act.at(f, f"a{HM - 1}"))
                    act.activation(Rw[:, :, :], Rw[:, :, :], ACT.Silu).then_inc(tail_act.sem, 1)
                if hs in (21, 22):
                    i = hs - 21
                    half = slice(i * HM // 2, (i + 1) * HM // 2)
                    act.wait_ge(tail_pool.sem, tail_pool.at(f, f"gated{i}"))
                    act.copy(Ghi[:, half, :], Rw[:, half, :]).then_inc(tail_act.sem, 1)
                if 24 <= hs < 32:
                    m = hs - 24
                    if m == 0:
                        act.wait_ge(tail_pool.sem, tail_pool.at(f, "lo0_1"))
                    act.wait_ge(tail_pe.sem, tail_pe.at(f, f"h1_{m}"))
                    act.activation(Rw[:, m, :], ring(1 - fp, f"h1_{m}")[:, 0, :], ACT.Copy,
                                   scale=c_("h1_s", m)).then_inc(tail_act.sem, 1)

            def gelu(g, layer, done, last):
                act.wait_ge(done.sem, done.at(g, last))
                act.activation(Rw[:, :, :], Rw[:, :, :], ACT.Gelu).then_inc(end_act.sem, 1)
                act.preload_act_table_set(LN_EXP)
                act.wait_ge(end_act.sem, end_act.at(g, f"gelu{layer}"))
                for i in range(2):
                    half = slice(i * HM // 2, (i + 1) * HM // 2)
                    act.copy(Ghi[:, half, :], Rw[:, half, :]).then_inc(end_act.sem, 1)

            def end_step(g, gp, hs):
                if hs == 0:
                    gelu(g, 1, tail_act, f"h1_{HM - 1}")
                if 2 <= hs < 10:
                    m = hs - 2
                    if m == 0:
                        act.wait_ge(end_pool.sem, end_pool.at(g, "lo1_1"))
                    act.wait_ge(end_pe.sem, end_pe.at(g, f"h2_{m}"))
                    act.activation(Rw[:, m, :], ring(gp, f"h2_{m}")[:, 0, :], ACT.Copy,
                                   scale=c_("h2_s", m)).then_inc(end_act.sem, 1)
                if hs == 10:
                    gelu(g, 2, end_act, f"h2_{HM - 1}")
                if hs == 14:
                    act.wait_ge(end_vec.sem, end_vec.at(g, "w"))
                    act.activation(fsm[:, 1, :], fsm[:, 0, :], ACT.Ln).then_inc(end_act.sem, 1)
                    act.wait_ge(end_act.sem, end_act.at(g, "ln"))
                    act.activation(fsm[:, 2, :], fsm[:, 1, :], ACT.Exp, scale=-0.5).then_inc(end_act.sem, 1)
                if hs == 15:
                    act.wait_ge(end_vec.sem, end_vec.at(g, "nmr"))
                    normed(fo, fo, fsm, 3).then_inc(end_act.sem, 1)

            def body(c, par, scan=False, head=False, tail=False, end=False, prepare=False,
                     seq_start=None, head_seq_start=None, j=None):
                for hs in range(HALVES):
                    n = hs // 2
                    if prepare and hs < len(STAGES):
                        round_stage(hs)
                    if prepare and 1 <= hs <= len(STAGES):
                        sum_stage(hs - 1)
                    if prepare and hs == HALVES - 2:
                        for i in range(2):
                            act.wait_ge(lo_stored[i], 16 * len(STAGES[i::2]))
                    if scan and n + 1 < N:
                        front(c, par, n + 1, hs % 2 == 0)
                    if head and hs >= HALVES - 2:
                        front(c + 1, 1 - par, 0, hs % 2 == 0)
                    if end:
                        end_step(c - 2, par, hs)
                    if tail:
                        tail_step(c - 1, 1 - par, hs)
                    if head:
                        head_step(c + 1, 1 - par, hs)
                    if hs == 19:
                        act.preload_act_table_set(LN_EXP)

            iterate(act, body)

        @block.vector
        def _(dve):
            start(dve, head_vec, scan_vec, tail_vec, end_vec)
            dve.memset(carry[:, :, :], 0.0).then_inc(carry_clear, 1)
            dve.wait_ge(carry_clear, 1)
            dve.wait_ge(ident_made, 3)
            dve.tensor_tensor(pick[:, :], ident[0:4 * N, 0:2 * N], ident[0:4 * N, 2 * N:4 * N],
                              ALU.add).then_inc(pick_made, 1)
            dve.wait_ge(small_in, 16 * SMALL)

            def left_of_stage(s):
                w, src, k = STAGES[s]
                n = SC // src.shape[1]
                dve.wait_ge(stage_hi, s + 1)
                if s >= 2:
                    dve.wait_ge(stage_abs, s - 1)
                    dve.wait_ge(lo_stored[s % 2], 16 * (s // 2))
                dve.tensor_tensor(dA_flat[s % 2].rearrange("p (k n) -> p k n", k=n),
                                  S_flat[s % 3].rearrange("p (k n) -> p k n", k=n),
                                  w[:, k:k + n, :].bitcast(F32), ALU.subtract).then_inc(stage_lo, 1)

            def newton(steps, c, names, sm, src, y):
                w, l, g = sm[:, src, :], sm[:, src + 1, :], sm[:, src + 2, :]
                dve.tensor_tensor(l, g, g, ALU.mult).then_inc(steps.sem, 1)
                dve.wait_ge(steps.sem, steps.at(c, names[0]))
                dve.tensor_tensor(l, l, w, ALU.mult).then_inc(steps.sem, 1)
                dve.wait_ge(steps.sem, steps.at(c, names[1]))
                dve.tensor_scalar(l, l, -0.5, 1.5, ALU.mult, ALU.add).then_inc(steps.sem, 1)
                dve.wait_ge(steps.sem, steps.at(c, names[2]))
                dve.tensor_tensor(y, g, l, ALU.mult).then_inc(steps.sem, 1)
                dve.wait_ge(steps.sem, steps.at(c, names[3]))

            def stats(steps, c, names, src, stat, mv, w):
                for t in range(TT):
                    a = dve.bn_stats(stat[:, t, :], src[:, t, :])
                a.then_inc(steps.sem, 1)
                dve.wait_ge(steps.sem, steps.at(c, names[0]))
                dve.memset(gate[:, :], 0.0)
                for t in range(TT):
                    a = dve.bn_aggr(mv[:, t, :], stat[:, t, :])
                a.then_inc(steps.sem, 1)
                dve.wait_ge(steps.sem, steps.at(c, names[1]))
                dve.tensor_scalar(w, mv[:, :, 1], LN_EPS, None, ALU.add).then_inc(steps.sem, 1)

            def minus_mean(dst, mv, r):
                return dve.scalar_tensor_tensor(dst, mv[:, :, 0], -1.0, r, ALU.mult, ALU.mult)

            def back(c, par, n, first):
                s = S[slot(par, n)]
                if first:
                    dve.wait_ge(scan_pool.sem, scan_pool.at(c, f"dBu{n}"))
                for d in ((0, 1) if first else (2, 3)):
                    dve.wait_ge(scan_act.sem, scan_act.at(c, f"e{d}_{n}"))
                    dve.tensor_tensor_scan(s[:, d, :], dA[n % 2][:, d, :], s[:, d, :],
                                           carry[:, n, d:d + 1], ALU.mult, ALU.add).then_inc(scan_vec.sem, 1)
                if not first:
                    dve.wait_ge(scan_vec.sem, scan_vec.at(c, f"s{DT - 1}_{n}"))
                    dve.tensor_copy(carry[:, n, :], s[:, :, T - 1]).then_inc(scan_vec.sem, 1)
                    dve.wait_ge(scan_vec.sem, scan_vec.at(c, f"carry{n}"))
                    dve.wait_ge(bcast_pe.sem, bcast_pe.at(c, f"b{n}"))
                    dve.tensor_tensor(s[:, :, :], s[:, :, :], bP[n % 2][:, 1:2, :].broadcast_to([P, DT, T]),
                                      ALU.mult).then_inc(scan_vec.sem, 1)

            def head_step(h, hp, hs, first):
                if hs == 1:
                    dve.wait_ge(xh_in.sem, xh_in.at(h, "landed"))
                    stats(head_vec, h, ("x_stats", "x_aggr"), xh, hstat, hmv, hsm[:, 0, :])
                if hs == 2:
                    r1 = mr[hp][:, 0, :]
                    dve.wait_ge(head_act.sem, head_act.at(h, "ex1"))
                    newton(head_vec, h, ("n1", "n2", "n3", "r1"), hsm, 0, r1)
                    dve.tensor_tensor(hsm[:, 5, :], r1, r1, ALU.mult).then_inc(head_vec.sem, 1)
                    dve.wait_ge(head_vec.sem, head_vec.at(h, "q1"))
                    dve.tensor_tensor(hsm[:, 5, :], hsm[:, 5, :], hmv[:, :, 1], ALU.mult).then_inc(head_vec.sem, 1)
                    dve.wait_ge(head_vec.sem, head_vec.at(h, "q2"))
                    dve.tensor_scalar(hsm[:, 6, :], hsm[:, 5, :], RMS_EPS, None, ALU.add).then_inc(head_vec.sem, 1)
                    minus_mean(mr[hp][:, 1, :], hmv, r1).then_inc(head_vec.sem, 1)
                if hs == 3:
                    dve.wait_ge(head_act.sem, head_act.at(h, "ex2"))
                    newton(head_vec, h, ("m1", "m2", "m3", "r2"), hsm, 6, hsm[:, 9, :])
                    dve.tensor_tensor(hsm[:, 12, :], mr[hp][:, 0, :], hsm[:, 9, :], ALU.mult).then_inc(head_vec.sem, 1)
                    dve.wait_ge(head_vec.sem, head_vec.at(h, "r12"))
                    minus_mean(hsm[:, 13, :], hmv, hsm[:, 12, :]).then_inc(head_vec.sem, 1)
                if hs == 7:
                    ahead, last = u_ext[:, :, 0:CONV - 1], u_ext[:, :, T:T + CONV - 1]
                    if isinstance(first, bool):
                        if first:
                            dve.memset(ahead, 0.0).then_inc(head_vec.sem, 1)
                        else:
                            dve.tensor_copy(ahead, last).then_inc(head_vec.sem, 1)
                    else:
                        with dve.If(first):
                            dve.memset(ahead, 0.0).then_inc(head_vec.sem, 1)
                        with dve.Else():
                            dve.tensor_copy(ahead, last).then_inc(head_vec.sem, 1)
                if hs in (11, 12, 13):
                    if hs == 11:
                        dve.wait_ge(head_act.sem, head_act.at(h, "cbase"))
                    for k in (hs - 11,):
                        for d in range(DT):
                            a = dve.scalar_tensor_tensor(uc[hp][:, d, :], u_ext[:, d, k:k + T],
                                                         c_("conv_w", d * CONV + k), uc[hp][:, d, :],
                                                         ALU.mult, ALU.add)
                        a.then_inc(head_vec.sem, 1)
                        dve.wait_ge(head_vec.sem, head_vec.at(h, f"tap{k}"))
                if hs == 22:
                    dve.wait_ge(head_act.sem, head_act.at(h, "dtx"))
                    dve.tensor_copy(BC[hp][:, :], hP[1][0:4 * N, 0, :]).then_inc(head_vec.sem, 1)
                    dve.wait_ge(head_vec.sem, head_vec.at(h, "bc_hi"))
                    lo = slice(2 * N, 4 * N)
                    dve.tensor_tensor(BC[hp][lo, :], hP[1][lo, 0, :], BC[hp][lo, :].bitcast(F32),
                                      ALU.subtract).then_inc(head_vec.sem, 1)
                if hs == 25:
                    dve.wait_ge(head_act.sem, head_act.at(h, "e"))
                    dve.wait_ge(tail_pool.sem, tail_pool.at(h - 2, "gated0"))
                    dve.tensor_scalar(X[hp][:, :, :], e_sp[:, :, :], 1.0, -1.0,
                                      ALU.add, ALU.add).then_inc(head_vec.sem, 1)

            def tail_step(f, fp, hs, head):
                if hs == 1:
                    dve.tensor_copy(mr_tail[:, :, :], mr[fp][:, :, :]).then_inc(tail_vec.sem, 1)
                    dve.wait_ge(sum_pe.sem, sum_pe.at(f, f"y{N - 1}"))
                    for d in range(DT):
                        a = dve.scalar_tensor_tensor(uc[fp][:, d, :], uc[fp][:, d, :], c_("D", d), yP[:, d, :],
                                                     ALU.mult, ALU.add)
                    a.then_inc(tail_vec.sem, 1)
                    dve.wait_ge(tail_vec.sem, tail_vec.at(f, "y_d"))
                    dve.tensor_tensor(z[fp][:, :, :], uc[fp][:, :, :], z[fp][:, :, :],
                                      ALU.mult).then_inc(tail_vec.sem, 1)
                if hs == 5:
                    dve.wait_ge(tail_vec.sem, tail_vec.at(f, "mr"))
                    dve.wait_ge(xt_in.sem, xt_in.at(f, "landed"))
                    dve.wait_ge(tail_pe.sem, tail_pe.at(f, "out"))
                    for t in range(TT):
                        a = dve.scalar_tensor_tensor(o[:, t, :], xt[:, t, :], mr_tail[:, 0, t:t + 1],
                                                     ring(1 - fp, "out")[:, t, :], ALU.mult, ALU.add)
                    a.then_inc(tail_vec.sem, 1)
                    dve.wait_ge(tail_vec.sem, tail_vec.at(f, "o_mul"))
                    for t in range(TT):
                        a = dve.tensor_scalar(o[:, t, :], o[:, t, :], mr_tail[:, 1, t:t + 1], None, ALU.add)
                    a.then_inc(tail_vec.sem, 1)
                    dve.wait_ge(tail_vec.sem, tail_vec.at(f, "o_add"))
                    stats(tail_vec, f, ("o_stats", "o_aggr"), o, tstat, tmv, tsm[:, 0, :])
                if hs == 6:
                    dve.wait_ge(tail_act.sem, tail_act.at(f, "o_ex"))
                    newton(tail_vec, f, ("o_n1", "o_n2", "o_n3", "o_r"), tsm, 0, tsm[:, 3, :])
                    minus_mean(tsm[:, 4, :], tmv, tsm[:, 3, :]).then_inc(tail_vec.sem, 1)
                if hs == 7:
                    dve.wait_ge(tail_act.sem, tail_act.at(f, "o_norm"))
                    dve.wait_ge(out_stored.sem, out_stored.at(f - 2, "landed"))
                    dve.tensor_tensor(x1[fp][:, :, :], xt[:, :, :], o[:, :, :], ALU.add).then_inc(tail_vec.sem, 1)
                    dve.wait_ge(tail_vec.sem, tail_vec.at(f, "x1"))
                    stats(tail_vec, f, ("x_stats", "x_aggr"), x1[fp], tstat, tmv, tsm[:, 5, :])
                if hs == 8:
                    dve.wait_ge(tail_act.sem, tail_act.at(f, "x_ex"))
                    newton(tail_vec, f, ("x_n1", "x_n2", "x_n3", "x_r"), tsm, 5, tsm[:, 8, :])
                    minus_mean(tsm[:, 9, :], tmv, tsm[:, 8, :]).then_inc(tail_vec.sem, 1)
                if hs == 14:
                    dve.wait_ge(tail_act.sem, tail_act.at(f, "xf_hi"))
                    dve.tensor_tensor(xfT_lo, ring(1 - fp, "xfT")[:, :, :], xfT_hi.bitcast(F32),
                                      ALU.subtract).then_inc(tail_vec.sem, 1)
                if 15 <= hs < 19:
                    for m in (2 * hs - 30, 2 * hs - 29):
                        if m == HM // 2 and head:
                            dve.wait_ge(head_pe.sem, head_pe.at(f + 2, "z1"))
                        dve.wait_ge(tail_act.sem, tail_act.at(f, f"a{m}"))
                        dve.tensor_scalar((X[fp], e_sp)[m // DT][:, m % DT, :], ring(1 - fp, f"ab{m}")[:, 1, :],
                                          c_("w2_s", m), None, ALU.mult).then_inc(tail_vec.sem, 1)

            def end_step(g, gp, hs):
                if hs == 14:
                    dve.wait_ge(end_pe.sem, end_pe.at(g, "w3"))
                    dve.tensor_tensor(fo[:, :, :], ring(gp, "w3")[:, :, :],
                                      s_3[:, None, :].broadcast_to([P, TT, DM]), ALU.mult).then_inc(end_vec.sem, 1)
                    dve.wait_ge(end_vec.sem, end_vec.at(g, "out"))
                    stats(end_vec, g, ("stats", "aggr"), fo, fstat, fmv, fsm[:, 0, :])
                if hs == 15:
                    dve.wait_ge(end_act.sem, end_act.at(g, "ex"))
                    newton(end_vec, g, ("n1", "n2", "n3", "r"), fsm, 0, fsm[:, 3, :])
                    minus_mean(fsm[:, 4, :], fmv, fsm[:, 3, :]).then_inc(end_vec.sem, 1)
                if hs == 16:
                    dve.wait_ge(end_act.sem, end_act.at(g, "norm"))
                    dve.tensor_tensor(x1[gp][:, :, :], x1[gp][:, :, :], fo[:, :, :], ALU.add).then_inc(end_vec.sem, 1)

            def body(c, par, scan=False, head=False, tail=False, end=False, prepare=False,
                     seq_start=None, head_seq_start=None, j=None):
                if seq_start is not None:
                    with dve.If(seq_start):
                        dve.memset(carry[:, :, :], 0.0).then_inc(carry_clear, 1)
                    with dve.Else():
                        dve.memset(gate[:, :], 0.0).then_inc(carry_clear, 1)
                    dve.wait_ge(carry_clear, j + 2)
                for hs in range(HALVES):
                    if scan:
                        back(c, par, hs // 2, hs % 2 == 0)
                    if end:
                        end_step(c - 2, par, hs)
                    if tail:
                        tail_step(c - 1, 1 - par, hs, head)
                    if head:
                        head_step(c + 1, 1 - par, hs, prepare if head_seq_start is None else head_seq_start)
                    if prepare and hs < len(STAGES):
                        left_of_stage(hs)
                    if prepare and hs == len(STAGES):
                        dve.wait_ge(stage_abs, len(STAGES))
                        dve.tensor_reduce(lo_all[:, :], lo_sum[:, :], AX.X, ALU.add).then_inc(lo_added, 1)
                        dve.wait_ge(lo_total, 1)
                        dve.tensor_scalar(inexact[:, :], fP[0][0:1, 0, 0:1], 0.0, None,
                                          ALU.is_gt).then_inc(lo_added, 1)

            iterate(dve, body)


def kernel(**inputs):
    import numpy as _np
    import concourse.bacc as _bacc
    from concourse import mybir as _mybir
    from concourse.bass_utils import run_bass_kernel_spmd as _run

    p = 128
    a = {k: _np.asarray(v) for k, v in inputs.items()}
    A, F = "L0_attn_", "L0_ffn_"

    def tiles(v):
        return v.reshape(v.shape[0] // p, p, -1).transpose(1, 0, 2).reshape(p, -1)

    arrays = {
        "x": a[A + "x"],
        "in_proj": a[A + "in_proj_w"].T, "x_proj": a[A + "x_proj_w"].T,
        "dt_proj": a[A + "dt_proj_w"].T, "out_proj": a[A + "out_proj_w"].T,
        "w1": a[F + "w1_w"].T, "w2": a[F + "w2_w"].T,
        "h1": a[F + "h1_w"].T, "h2": a[F + "h2_w"].T, "w3": a[F + "w3_w"].T,
        "cols": _np.concatenate([tiles(a[k]) for k in (
            A + "conv_w", A + "conv_b", A + "dt_proj_b", A + "D", A + "A_log", A + "norm_w",
            F + "w1_s", F + "w2_s", F + "h1_s", F + "h2_s")], axis=1),
        "w3_s": a[F + "w3_s"],
    }
    arrays = {f"in_{k}": _np.ascontiguousarray(v) for k, v in arrays.items()}
    nc = _bacc.Bacc("TRN2", target_bir_lowering=False, num_devices=1)
    args = [nc.dram_tensor(k, v.shape, _mybir.dt.from_np(v.dtype), kind="ExternalInput").ap()
            for k, v in arrays.items()]
    args.append(nc.dram_tensor("out_0", a[A + "x"].shape, _mybir.dt.float32, kind="ExternalOutput").ap())
    build(nc, *args)
    r = _run(nc, [arrays], core_ids=[0])
    return r.results[0]["out_0"]
```

```python
from contextlib import ExitStack

import concourse.bass as bass
from concourse import mybir

ALU = mybir.AluOpType
ACT = mybir.ActivationFunctionType
AX = mybir.AxisListType
F32 = mybir.dt.float32
F32R = mybir.dt.float32r
I32 = mybir.dt.int32

P = 128
T = 256
TT = T // P
LN_EPS = 1e-5
RMS_EPS = 1.1920928955078125e-07
LN_EXP = "natural_log_exp_and_others"


class Steps:

    def __init__(self, sem, names):
        self.sem, self.names = sem, list(names)
        self.per_chunk = len(self.names)

    def at(self, chunk, name):
        return chunk * self.per_chunk + (2 * self.per_chunk + self.names.index(name) + 1)

    def piece(self, chunk, index):
        return chunk * (16 * self.per_chunk) + index * 16 + (2 * self.per_chunk + 1) * 16


def build(nc, x, in_proj, x_proj, dt_proj, out_proj, w1, w2, h1, h2, w3, cols, w3_s, out):
    B, L, DM = x.shape
    R, DI = dt_proj.shape
    N = (x_proj.shape[1] - R) // 2
    HID = w1.shape[1]
    CONV = 4
    DT, KM, HM = DI // P, DM // P, HID // P
    CHUNKS = B * L // T
    PER_SEQ = L // T
    assert B == 2 and PER_SEQ % 2 == 0 and N % 2 == 0 and (DT, KM, HM, TT) == (4, 2, 8, 2) and DM == T

    at, col_at = 0, {}
    for name, width in (("conv_w", DT * CONV), ("conv_b", DT), ("dt_b", DT), ("D", DT), ("A_log", DT * N),
                        ("norm_w", KM), ("w1_s", HM), ("w2_s", HM), ("h1_s", HM), ("h2_s", HM)):
        col_at[name] = at
        at += width
    COLS = at

    x_in = x.rearrange("b (c t p) d -> (b c) p t d", t=TT, p=P)
    x_out = out.rearrange("b (c t p) d -> (b c) p t d", t=TT, p=P)

    ctx = ExitStack()
    with ctx:
        def sb(name, shape, dt=F32):
            return ctx.enter_context(nc.sbuf_tensor(name, shape, dt))

        def pb(name, shape):
            return ctx.enter_context(nc.psum_tensor(name, shape, F32))

        def sem(name):
            return ctx.enter_context(nc.semaphore(name))

        w_in = sb("w_in", [P, KM, 2 * DI])
        XC = 4 * N + R
        w_x = sb("w_x", [P, DT, XC])
        w_dt = sb("w_dt", [XC, DI])[4 * N:XC, :]
        w_out = sb("w_out", [P, DT, DM])
        w_1 = sb("w_1", [P, KM, HID], F32R)
        w_2 = sb("w_2", [P, KM, HID], F32R)
        w_h1 = sb("w_h1", [P, HM, HID], F32R)
        w_h2 = sb("w_h2", [P, HM, HID], F32R)
        w_3 = sb("w_3", [P, HM, DM], F32R)
        s_3 = sb("s_3", [P, DM])
        col = sb("col", [P, COLS])
        A = sb("A", [P, DT * N])
        ident = sb("ident", [P, P])
        ones = sb("ones", [P, 1])
        pick = sb("pick", [4 * N, 2 * N], F32R)

        xh = sb("xh", [P, TT, DM])
        u_ext = sb("u_ext", [P, DT, CONV - 1 + T])
        uc = [sb(f"uc{i}", [P, DT, T]) for i in range(2)]
        z = [sb(f"z{i}", [P, DT, T]) for i in range(2)]
        delta = [sb(f"delta{i}", [P, DT, T]) for i in range(2)]
        X = [sb(f"X{i}", [P, DT, T]) for i in range(2)]
        BC = [sb(f"BC{i}", [4 * N, T], F32R) for i in range(2)]
        e_sp = sb("e_sp", [P, DT, T])
        hn = e_sp[:, 0:2, :]
        hT = e_sp[:, 2:4, :]
        dtx = e_sp[4 * N:XC, 3, :]
        hstat = sb("hstat", [P, TT, 6])
        hmv = sb("hmv", [P, TT, 2])
        hsm = sb("hsm", [P, 14, TT])

        dA = [sb(f"dA{i}", [P, DT, T]) for i in range(2)]
        Bs = sb("Bs", [P, T])
        Cs = sb("Cs", [P, T])
        S = [sb(f"S{i}", [P, DT, T]) for i in range(3)]
        gate = sb("gate", [P, 1])
        carry = sb("carry", [P, N, DT])

        xt = sb("xt", [P, TT, DM])
        o = sb("o", [P, TT, DM])
        x1_both = sb("x1", [P, 2, TT, DM])
        x1 = [x1_both[:, i, :, :] for i in range(2)]
        xf_hi = sb("xf_hi", [P, KM, T], F32R)
        Rw = sb("Rw", [P, HM, T])
        Ghi = sb("Ghi", [P, HM, T], F32R)
        Glo = sb("Glo", [P, HM, T], F32R)
        xfT_hi, xfT_lo = xf_hi[:, :, :], Glo[:, 0:KM, :]
        mr = [sb(f"mr{i}", [P, 2, TT]) for i in range(2)]
        tstat = sb("tstat", [P, TT, 6])
        tmv = sb("tmv", [P, TT, 2])
        tsm = sb("tsm", [P, 10, TT])
        fstat = sb("fstat", [P, TT, 6])
        fmv = sb("fmv", [P, TT, 2])
        fsm = sb("fsm", [P, 5, TT])

        SC = HID
        w_piece = sb("w_piece", [P, 2 * P])
        STAGES = [(w, src, k) for w, src, n in ((w_1, w1, KM), (w_2, w2, KM), (w_h1, h1, HM), (w_h2, h2, HM))
                  for k in range(n)] + [(w_3, w3, k) for k in range(0, HM, SC // DM)]
        inexact = sb("inexact", [1, 1])
        some_inexact = sb("some_inexact", [1, 1], I32)
        LAYER_PIECES = HM * HM // 2
        TAIL_PIECES = 2 * HM + LAYER_PIECES
        END_PIECES = LAYER_PIECES + TT * HM

        yP = pb("yP", [P, DT, T])
        bP = [pb(f"bP{i}", [P, 2, T]) for i in range(2)]
        hP = [pb(f"hP{i}", [P, 2, T]) for i in range(2)]
        fP = [pb(f"fP{i}", [P, 2, T]) for i in range(2)]

        def c_(name, i, n=1):
            return col[:, col_at[name] + i:col_at[name] + i + n]

        head_vec = Steps(sem("head_vec"),
                         ["x_stats", "x_aggr", "w", "n1", "n2", "r1", "q1", "q2", "w2", "nmr1",
                          "m1", "m2", "r2", "r12", "nmr12", "halo", "tap0", "tap1", "tap2",
                          "bc_hi", "bc_lo", "t1", "res", "delta"])
        scan_vec = Steps(sem("scan_vec"),
                         [f"{k}{n}" for n in range(N) for k in ("s0_", "s1_", "s2_", "s3_", "carry", "g")])
        tail_vec = Steps(sem("tail_vec"),
                         ["y_d", "yz", "o_mul", "o_add", "o_stats", "o_aggr", "o_w", "o_n1", "o_n2",
                          "o_r", "o_nmr", "x1", "x_stats", "x_aggr", "x_w", "x_n1", "x_n2", "x_r",
                          "x_nmr", "xf_lo"] + [f"b{m}" for m in range(HM)] + ["gated0", "gated1", "hi0_1", "lo0_1"])
        end_vec = Steps(sem("end_vec"),
                        ["hi1_1", "lo1_1", "hi2_1", "lo2_1", "out", "stats", "aggr", "w", "n1", "n2", "r",
                         "nmr", "sum"])
        head_act = Steps(sem("head_act"),
                         ["ln1", "ex1", "ln2", "ex2", "hn", "hT", "u0", "u1", "cbase", "silu", "z0", "z1",
                          "dtx", "v0", "v1", "e", "l"])
        scan_act = Steps(sem("scan_act"),
                         [f"{k}{n}" for n in range(N) for k in ("b", "e0_", "e1_", "e2_", "e3_", "c")])
        tail_act = Steps(sem("tail_act"),
                         ["o_ln", "o_ex", "o_norm", "x_ln", "x_ex", "xf", "xf_hi"] + [f"a{m}" for m in range(HM)]
                         + ["silu0", "silu1", "hi0_0"] + [f"h1_{m}" for m in range(HM)] + ["gelu1_0", "hi1_0", "gelu1_1"])
        end_act = Steps(sem("end_act"), [f"h2_{m}" for m in range(HM)] + ["gelu2_0", "hi2_0", "gelu2_1", "ln", "ex", "norm"])
        head_pe = Steps(sem("head_pe"), ["hT", "u0", "u1", "z0", "z1", "xp", "d0", "d1"])
        bcast_pe = Steps(sem("bcast_pe"), [f"b{n}" for n in range(N)])
        sum_pe = Steps(sem("sum_pe"), [f"y{n}" for n in range(N)])
        tail_pe = Steps(sem("tail_pe"),
                        ["out", "xfT"] + [f"{branch}{i}" for i in range(HM // 2) for branch in "ab"]
                        + [f"h1_{m}" for m in range(HM)])
        end_pe = Steps(sem("end_pe"), [f"h2_{m}" for m in range(HM)] + ["w3"])
        head_pool = Steps(sem("head_pool"), ["log1p", "X"])
        scan_pool = Steps(sem("scan_pool"), [f"dBu{n}" for n in range(N)])
        tail_pool = Steps(sem("tail_pool"), ["lo0_0"])
        end_pool = Steps(sem("end_pool"), ["lo1_0", "lo2_0"])
        xh_in = Steps(sem("xh_in"), ["dma"] * 15 + ["landed"])
        xt_in = Steps(sem("xt_in"), ["dma"] * 15 + ["landed"])
        out_stored = Steps(sem("out_stored"), ["dma"] * 15 + ["landed"])
        tail_piece_in = Steps(sem("tail_piece_in"), range(TAIL_PIECES))
        tail_piece_used = Steps(sem("tail_piece_used"), range(TAIL_PIECES))
        end_piece_in = Steps(sem("end_piece_in"), range(END_PIECES))
        end_piece_used = Steps(sem("end_piece_used"), range(END_PIECES))

        cols_in = sem("cols_in")
        small_in = sem("small_in")
        late_in = sem("late_in")
        stage_in = [sem(f"stage_in{i}") for i in range(3)]
        stage_hi = sem("stage_hi")
        stage_marked = sem("stage_marked")
        stage_counted = sem("stage_counted")
        flag_set = sem("flag_set")
        ident_made = sem("ident_made")
        pick_made = sem("pick_made")
        A_made = sem("A_made")
        carry_clear = sem("carry_clear")

        SMALL, LATE = 5, 2
        staging = [Rw[:, i * HM // 2:(i + 1) * HM // 2, :].rearrange("p a b -> p (a b)") for i in range(2)]
        staging.append(x1_both[:, :, :, :].rearrange("p i t d -> p (i t d)"))
        counts = fP[0][0:1, :, :].rearrange("p a b -> p (a b)")

        def start(eng, *steps):
            for s in steps:
                eng.sem_inc(s.sem, 2 * s.per_chunk)

        def iterate(engine, body):
            body(-1, 1, head=True, prepare=True)
            body(0, 0, scan=True, head=True)
            body(1, 1, scan=True, head=True, tail=True)
            with engine.Fori(0, CHUNKS // 2 - 2) as j:
                body(j * 2 + 2, 0, scan=True, head=True, tail=True, end=True,
                     seq_start=(j * 2 == PER_SEQ - 2), j=j)
                body(j * 2 + 3, 1, scan=True, head=True, tail=True, end=True,
                     head_seq_start=(j * 2 == PER_SEQ - 4))
            body(CHUNKS - 2, 0, scan=True, head=True, tail=True, end=True)
            body(CHUNKS - 1, 1, scan=True, tail=True, end=True)
            body(CHUNKS, 0, tail=True, end=True)
            body(CHUNKS + 1, 1, end=True)

        HALVES = 2 * N

        def stages_at(c, hs):
            if not isinstance(c, int) or c > 0:
                return []
            return [s for s in range(len(STAGES))
                    if (c, hs) == ((-1, (20, 22, 27, 29)[s]) if s < 4 else (0, 1 + (s - 4) * 8 // 5))]

        def slot(par, n):
            return (n + par) % 3

        def slot_before(c, par, n):
            for m in range(n - 1, -1, -1):
                if slot(par, m) == slot(par, n):
                    return c, f"y{m}"
            for m in range(N - 1, -1, -1):
                if slot(1 - par, m) == slot(par, n):
                    return c - 1, f"y{m}"

        USES = (["out"] + [f"h2_{m}" for m in range(HM)] + ["xfT", "w3"]
                + [f"{branch}{i}" for i in range(HM // 2) for branch in "ab"] + [f"h1_{m}" for m in range(HM)])

        def ring(par, use):
            return fP[(par + USES.index(use)) % 2]

        def last_reader(c, use, tail=True, end=True):
            def reader(c, name):
                if name == "out":
                    return tail_vec, c - 1, "o_mul"
                if name == "xfT":
                    return tail_vec, c - 1, "xf_lo"
                if name == "w3":
                    return end_vec, c - 2, "out"
                if name.startswith("h2"):
                    return end_act, c - 2, name
                if name.startswith("h1"):
                    return tail_act, c - 1, name
                return (tail_act if name[0] == "a" else tail_vec), c - 1, f"{name[0]}{2 * int(name[1:]) + 1}"
            assert len(USES) % 2 == 1
            at = USES.index(use) - 2
            while at >= 0:
                of_end = USES[at] == "w3" or USES[at].startswith("h2")
                if end if of_end else tail:
                    return reader(c, USES[at])
                at -= 2
            return reader(c - 1, USES[at + len(USES)])

        block = ctx.enter_context(nc.Block())

        @block.sync
        def _(sp):
            start(sp, xh_in, xt_in, out_stored, tail_piece_in, end_piece_in)
            sp.sem_inc(tail_piece_in.sem, 30 * TAIL_PIECES)
            sp.sem_inc(end_piece_in.sem, 30 * END_PIECES)
            sp.dma_start(xh[:, :, :], x_in[0]).then_inc(xh_in.sem, 16)
            sp.dma_start(col[:, :], cols).then_inc(cols_in, 16)
            sp.dma_start(w_in[:, :, :], in_proj.rearrange("(k p) n -> p k n", p=P)).then_inc(small_in, 16)
            xp = x_proj.rearrange("(k p) n -> p k n", p=P)
            sp.dma_start(w_x[:, :, 4 * N:XC], xp[:, :, 0:R]).then_inc(small_in, 16)
            sp.dma_start(w_x[:, :, 0:2 * N], xp[:, :, R:R + 2 * N]).then_inc(small_in, 16)
            sp.dma_start(w_x[:, :, 2 * N:4 * N], xp[:, :, R:R + 2 * N]).then_inc(small_in, 16)
            sp.dma_start(w_dt, dt_proj).then_inc(small_in, 16)
            sp.dma_start(w_out[:, :, :], out_proj.rearrange("(k p) n -> p k n", p=P)).then_inc(late_in, 16)
            sp.dma_start(s_3[:, :], w3_s.partition_broadcast(P)).then_inc(late_in, 16)

            def load_stage(s):
                w, src, k = STAGES[s]
                if s >= 3:
                    sp.wait_ge(stage_counted, s - 2)
                rows = src.rearrange("(k p) n -> p k n", p=P)
                n = SC // src.shape[1]
                sp.dma_start(staging[s % 3].rearrange("p (k n) -> p k n", k=n), rows[:, k:k + n, :])\
                  .then_inc(stage_in[s % 3], 16)

            for s in range(3):
                load_stage(s)
            some_lo = [None]

            def tiles_of(layer):
                return layer.rearrange("(q k p) (m n) -> m q p k n", k=2, p=P, n=P)

            pairs = HM // 2
            piece = w_piece[:, :].rearrange("p (k n) -> p k n", k=2)

            def body(c, par, scan=False, head=False, tail=False, end=False, prepare=False,
                     seq_start=None, head_seq_start=None, j=None):
                if isinstance(c, int) and c == 1:
                    sp.wait_ge(flag_set, 2)
                    some_lo[0] = sp.value_load(some_inexact[0:1, 0:1], min_val=0, max_val=1)
                if end:
                    with sp.If(some_lo[0] != 0):
                        with sp.Fori(0, HM) as m:
                            for q in range(pairs):
                                sp.wait_ge(tail_piece_used.sem, tail_piece_used.at(c - 2, TAIL_PIECES - 1))
                                sp.wait_ge(end_piece_used.sem, end_piece_used.at(c - 2, 0) - 1 + q + m * pairs)
                                sp.dma_start(piece, tiles_of(h2)[m, q]).then_inc(end_piece_in.sem, 16)
                        for t in range(TT):
                            with sp.Fori(0, HM) as k:
                                sp.wait_ge(end_piece_used.sem,
                                           end_piece_used.at(c - 2, 0) - 1 + LAYER_PIECES + t * HM + k)
                                sp.dma_start(w_piece[:, :], w3.rearrange("(k p) n -> k p n", p=P)[k])\
                                  .then_inc(end_piece_in.sem, 16)
                    with sp.Else():
                        sp.nop()
                if tail:
                    with sp.If(some_lo[0] != 0):
                        with sp.Fori(0, HM // 2) as m:
                            for q, (w, t) in enumerate(((w1, 0), (w1, 1), (w2, 0), (w2, 1))):
                                sp.wait_ge(end_piece_used.sem, end_piece_used.at(c - 2, END_PIECES - 1))
                                sp.wait_ge(tail_piece_used.sem, tail_piece_used.at(c - 1, 0) - 1 + q + m * 4)
                                sp.dma_start(piece, tiles_of(w)[m * 2 + t, 0]).then_inc(tail_piece_in.sem, 16)
                        with sp.Fori(0, HM) as m:
                            for q in range(pairs):
                                sp.wait_ge(tail_piece_used.sem,
                                           tail_piece_used.at(c - 1, 2 * HM) - 1 + q + m * pairs)
                                sp.dma_start(piece, tiles_of(h1)[m, q]).then_inc(tail_piece_in.sem, 16)
                    with sp.Else():
                        sp.nop()
                if end:
                    sp.wait_ge(end_vec.sem, end_vec.at(c - 2, "sum"))
                    sp.dma_start(x_out[c - 2], x1[par][:, :, :]).then_inc(out_stored.sem, 16)
                if head and not (isinstance(c, int) and c + 2 >= CHUNKS):
                    sp.wait_ge(head_act.sem, head_act.at(c + 1, "hn"))
                    sp.dma_start(xh[:, :, :], x_in[c + 2]).then_inc(xh_in.sem, 16)
                if scan:
                    sp.wait_ge(tail_vec.sem, tail_vec.at(c - 1, "x1"))
                    sp.dma_start(xt[:, :, :], x_in[c]).then_inc(xt_in.sem, 16)
                if prepare:
                    for s in range(3, len(STAGES)):
                        load_stage(s)

            iterate(sp, body)
            sp.wait_ge(out_stored.sem, out_stored.at(CHUNKS - 1, "landed"))

        @block.gpsimd
        def _(pool):
            start(pool, head_pool, scan_pool, tail_pool, end_pool)
            pool.memset(ones[:, :], 1.0).then_inc(ident_made, 1)
            pool.memset(ident[:, :], 0.0).then_inc(ident_made, 1)
            pool.wait_ge(ident_made, 2)
            pool.affine_select(out=ident[:, :], in_=ident[:, :], compare_op=ALU.not_equal, fill=1.0,
                               base=0, pattern=[[-1, P]], channel_multiplier=1).then_inc(ident_made, 1)

            def front(c, par, n):
                pool.wait_ge(scan_act.sem, scan_act.at(c, f"b{n}"))
                if n == 0:
                    pool.wait_ge(head_pool.sem, head_pool.at(c, "X"))
                before, read = slot_before(c, par, n)
                pool.wait_ge(sum_pe.sem, sum_pe.at(before, read))
                pool.tensor_tensor(S[slot(par, n)][:, :, :], X[par][:, :, :],
                                   Bs[:, None, :].broadcast_to([P, DT, T]),
                                   ALU.mult).then_inc(scan_pool.sem, 1)

            def head_step(h, hp, hs):
                if hs == 27:
                    pool.wait_ge(head_vec.sem, head_vec.at(h, "res"))
                    pool.wait_ge(head_act.sem, head_act.at(h, "l"))
                    pool.tensor_tensor(X[hp][:, :, :], X[hp][:, :, :], e_sp[:, :, :],
                                       ALU.add).then_inc(head_pool.sem, 1)
                if hs == 29:
                    pool.wait_ge(head_vec.sem, head_vec.at(h, "delta"))
                    pool.tensor_tensor(X[hp][:, :, :], delta[hp][:, :, :], uc[hp][:, :, :],
                                       ALU.mult).then_inc(head_pool.sem, 1)

            def low_half(act_steps, c, name):
                half = slice(0, HM // 2)
                pool.wait_ge(act_steps.sem, act_steps.at(c, name))
                return pool.tensor_tensor(Glo[:, half, :], Rw[:, half, :], Ghi[:, half, :].bitcast(F32), ALU.subtract)

            def tail_step(f, fp, hs):
                if hs == 21:
                    low_half(tail_act, f, "hi0_0").then_inc(tail_pool.sem, 1)

            def end_step(g, gp, hs):
                if hs == 0:
                    low_half(tail_act, g, "hi1_0").then_inc(end_pool.sem, 1)
                if hs == 12:
                    low_half(end_act, g, "hi2_0").then_inc(end_pool.sem, 1)

            def body(c, par, scan=False, head=False, tail=False, end=False, prepare=False,
                     seq_start=None, head_seq_start=None, j=None):
                for hs in range(HALVES):
                    n = hs // 2
                    if scan and hs % 2 == 0 and n + 1 < N:
                        front(c, par, n + 1)
                    if head and hs == HALVES - 2:
                        front(c + 1, 1 - par, 0)
                    if end:
                        end_step(c - 2, par, hs)
                    if tail:
                        tail_step(c - 1, 1 - par, hs)
                    if head:
                        head_step(c + 1, 1 - par, hs)
            iterate(pool, body)

        @block.tensor
        def _(pe):
            start(pe, head_pe, bcast_pe, sum_pe, tail_pe, end_pe, tail_piece_used, end_piece_used)
            pe.wait_ge(ident_made, 3)
            pe.wait_ge(small_in, 16 * SMALL)
            pe.wait_ge(pick_made, 1)
            some_lo = [None]

            def products(dst, lhs, rhs, k):
                for i in range(k):
                    mm = pe.matmul(dst, lhs(i), rhs(i), start=(i == 0), stop=(i == k - 1))
                return mm

            def split_products(dst, w, cols_, hi, lo, k, used, landed, chunk, piece):
                for i in range(k):
                    if piece is None:
                        pe.matmul(dst, w[:, i, cols_], hi[:, i, :], start=(i == 0), stop=False)
                        mm = pe.matmul(dst, w[:, i, cols_], lo[:, i, :], start=False, stop=(i == k - 1))
                    else:
                        if i % 2 == 0:
                            pe.wait_ge(landed.sem, landed.piece(chunk, piece + i // 2))
                        part = w_piece[:, (i % 2) * P:(i % 2 + 1) * P]
                        pe.matmul(dst, part, hi[:, i, :].bitcast(F32), start=(i == 0), stop=False)
                        mm = pe.matmul(dst, part, lo[:, i, :].bitcast(F32), start=False, stop=(i == k - 1))
                        if i % 2 == 1:
                            mm.then_inc(used.sem, 1)
                if piece is not None:
                    pe.wait_ge(used.sem, used.at(chunk, piece + k // 2 - 1))
                    mm = pe.nop()
                return mm

            def bcast(c, par, n):
                if n == 0:
                    pe.wait_ge(head_vec.sem, head_vec.at(c, "bc_lo"))
                if n >= 2:
                    pe.wait_ge(scan_act.sem, scan_act.at(c, f"c{n - 2}"))
                else:
                    pe.wait_ge(scan_act.sem, scan_act.at(c - 1, f"c{N - 2 + n}"))
                for i, r in ((0, n), (1, N + n)):
                    mm = pe.matmul(bP[n % 2][:, i, :], pick[:, r:r + 1].broadcast_to([4 * N, P]), BC[par][:, :],
                                   start=True, stop=True)
                mm.then_inc(bcast_pe.sem, 1)

            def state_sum(c, par, n):
                pe.wait_ge(scan_vec.sem, scan_vec.at(c, f"g{n}"))
                if n == 0:
                    pe.wait_ge(tail_vec.sem, tail_vec.at(c - 1, "y_d"))
                for i in range(DT // 2):
                    mm = pe.matmul(yP[:, 2 * i:2 * i + 2, :], ident[:, :], S[slot(par, n)][:, 2 * i:2 * i + 2, :],
                                   start=(n == 0), stop=(n == N - 1))
                mm.then_inc(sum_pe.sem, 1)

            def head_step(h, hp, hs):
                if hs == 8:
                    pe.wait_ge(head_act.sem, head_act.at(h, "hn"))
                    pe.wait_ge(head_act.sem, head_act.at(h - 1, "v0"))
                    for k in range(KM):
                        for t in range(TT):
                            mm = pe.transpose(hP[0][:, k, t * P:(t + 1) * P], hn[:, t, k * P:(k + 1) * P],
                                              ident[:, :])
                    mm.then_inc(head_pe.sem, 1)
                if 10 <= hs < 14:
                    q = hs - 10
                    if q == 0:
                        pe.wait_ge(head_act.sem, head_act.at(h, "hT"))
                        pe.wait_ge(head_act.sem, head_act.at(h - 1, "v1"))
                    else:
                        pe.wait_ge(head_act.sem, head_act.at(h, ("hT", "u0", "u1")[q - 1]))
                    for d in range(2):
                        m = 2 * q + d
                        mm = products(hP[(q + 1) % 2][:, d, :], lambda k: w_in[:, k, m * P:(m + 1) * P],
                                      lambda k: hT[:, k, :], KM)
                    mm.then_inc(head_pe.sem, 1)
                if hs == 20:
                    pe.wait_ge(head_act.sem, head_act.at(h, "z0"))
                    products(hP[1][0:XC, 0, :], lambda k: w_x[:, k, :], lambda k: uc[hp][:, k, :],
                             DT).then_inc(head_pe.sem, 1)
                if hs == 22:
                    pe.wait_ge(head_act.sem, head_act.at(h, "dtx"))
                    for q in range(2):
                        if q == 1:
                            pe.wait_ge(head_vec.sem, head_vec.at(h, "bc_lo"))
                        for d in range(2):
                            m = 2 * q + d
                            mm = pe.matmul(hP[q][:, d, :], w_dt[:, m * P:(m + 1) * P], dtx, start=True, stop=True)
                        mm.then_inc(head_pe.sem, 1)

            def branch(f, fp, which, i, stream):
                name = f"{'ab'[which]}{i}"
                if name == "a0":
                    pe.wait_ge(tail_vec.sem, tail_vec.at(f, "xf_lo"))
                steps, chunk, reader = last_reader(f + 1, name)
                pe.wait_ge(steps.sem, steps.at(chunk, reader))
                for t in range(2):
                    m = 2 * i + t
                    mm = split_products(ring(1 - fp, name)[:, t, :], (w_1, w_2)[which], slice(m * P, (m + 1) * P),
                                        xfT_hi, xfT_lo, KM, tail_piece_used, tail_piece_in, f,
                                        4 * i + 2 * which + t if stream else None)
                mm.then_inc(tail_pe.sem, 1)

            def hidden1(f, fp, m, stream):
                if m == 0:
                    pe.wait_ge(tail_pool.sem, tail_pool.at(f, "lo0_0"))
                    pe.wait_ge(tail_vec.sem, tail_vec.at(f, "lo0_1"))
                steps, chunk, name = last_reader(f + 1, f"h1_{m}")
                pe.wait_ge(steps.sem, steps.at(chunk, name))
                piece = 2 * HM + m * (HM // 2)
                split_products(ring(1 - fp, f"h1_{m}")[:, 0, :], w_h1, slice(m * P, (m + 1) * P), Ghi, Glo, HM,
                               tail_piece_used, tail_piece_in, f, piece if stream else None).then_inc(tail_pe.sem, 1)

            def hidden2(g, gp, m, stream, tail):
                if m == 0:
                    pe.wait_ge(end_pool.sem, end_pool.at(g, "lo1_0"))
                    pe.wait_ge(end_vec.sem, end_vec.at(g, "lo1_1"))
                steps, chunk, name = last_reader(g + 2, f"h2_{m}", tail=tail)
                pe.wait_ge(steps.sem, steps.at(chunk, name))
                split_products(ring(gp, f"h2_{m}")[:, 0, :], w_h2, slice(m * P, (m + 1) * P), Ghi, Glo, HM,
                               end_piece_used, end_piece_in, g, m * (HM // 2) if stream else None).then_inc(end_pe.sem, 1)

            def last_product(g, gp, stream, tail):
                pe.wait_ge(end_pool.sem, end_pool.at(g, "lo2_0"))
                pe.wait_ge(end_vec.sem, end_vec.at(g, "lo2_1"))
                steps, chunk, name = last_reader(g + 2, "w3", tail=tail)
                pe.wait_ge(steps.sem, steps.at(chunk, name))
                for t in range(TT):
                    dst = ring(gp, "w3")[:, t, :]
                    tok = slice(t * P, (t + 1) * P)
                    for k in range(HM):
                        if not stream:
                            pe.matmul(dst, Ghi[:, k, tok], w_3[:, k, :], start=(k == 0), stop=False)
                            mm = pe.matmul(dst, Glo[:, k, tok], w_3[:, k, :], start=False, stop=(k == HM - 1))
                        else:
                            pe.wait_ge(end_piece_in.sem, end_piece_in.piece(g, LAYER_PIECES + t * HM + k))
                            pe.matmul(dst, Ghi[:, k, tok].bitcast(F32), w_piece[:, :], start=(k == 0), stop=False)
                            pe.matmul(dst, Glo[:, k, tok].bitcast(F32), w_piece[:, :], start=False,
                                      stop=(k == HM - 1)).then_inc(end_piece_used.sem, 1)
                if stream:
                    pe.wait_ge(end_piece_used.sem, end_piece_used.at(g, END_PIECES - 1))
                    mm = pe.nop()
                mm.then_inc(end_pe.sem, 1)

            def tail_step(f, fp, hs):
                if hs == 2:
                    pe.wait_ge(tail_vec.sem, tail_vec.at(f, "yz"))
                    steps, chunk, name = last_reader(f + 1, "out")
                    pe.wait_ge(steps.sem, steps.at(chunk, name))
                    for t in range(TT):
                        mm = products(ring(1 - fp, "out")[:, t, :], lambda k: z[fp][:, k, t * P:(t + 1) * P],
                                      lambda k: w_out[:, k, :], DT)
                    mm.then_inc(tail_pe.sem, 1)
                if hs == 11:
                    pe.wait_ge(tail_act.sem, tail_act.at(f, "xf"))
                    steps, chunk, name = last_reader(f + 1, "xfT")
                    pe.wait_ge(steps.sem, steps.at(chunk, name))
                    for k in range(KM):
                        for t in range(TT):
                            mm = pe.transpose(ring(1 - fp, "xfT")[:, k, t * P:(t + 1) * P],
                                              o[:, t, k * P:(k + 1) * P], ident[:, :])
                    mm.then_inc(tail_pe.sem, 1)
                if 15 <= hs < 19:
                    with pe.If(some_lo[0] != 0):
                        for which in range(2):
                            branch(f, fp, which, hs - 15, True)
                    with pe.Else():
                        for which in range(2):
                            branch(f, fp, which, hs - 15, False)
                if 23 <= hs < 31:
                    with pe.If(some_lo[0] != 0):
                        hidden1(f, fp, hs - 23, True)
                    with pe.Else():
                        hidden1(f, fp, hs - 23, False)

            def end_step(g, gp, hs, tail):
                if 3 <= hs < 11:
                    with pe.If(some_lo[0] != 0):
                        hidden2(g, gp, hs - 3, True, tail)
                    with pe.Else():
                        hidden2(g, gp, hs - 3, False, tail)
                if hs == 14:
                    with pe.If(some_lo[0] != 0):
                        last_product(g, gp, True, tail)
                    with pe.Else():
                        last_product(g, gp, False, tail)

            def body(c, par, scan=False, head=False, tail=False, end=False, prepare=False,
                     seq_start=None, head_seq_start=None, j=None):
                for hs in range(HALVES):
                    n = hs // 2
                    if hs % 2 == 1:
                        if scan and n + 2 < N:
                            bcast(c, par, n + 2)
                        if head and n + 2 >= N:
                            bcast(c + 1, 1 - par, n + 2 - N)
                        if scan and n > 0:
                            state_sum(c, par, n - 1)
                    if tail and hs == 0:
                        state_sum(c - 1, 1 - par, N - 1)
                    if end:
                        end_step(c - 2, par, hs, tail)
                    if tail:
                        tail_step(c - 1, 1 - par, hs)
                    if head:
                        head_step(c + 1, 1 - par, hs)
                    if prepare and hs == HALVES - 1:
                        pe.wait_ge(late_in, 16 * LATE)
                    for s in stages_at(c, hs - 1):
                        pe.wait_ge(stage_marked, s + 1)
                        for i in range(2):
                            mm = pe.matmul(counts, ones[:, :], staging[s % 3][:, i * 2 * T:(i + 1) * 2 * T],
                                           start=(s == 0 and i == 0), stop=(s == len(STAGES) - 1 and i == 1))
                        mm.then_inc(stage_counted, 1)
                    if isinstance(c, int) and c == 1 and hs == 0:
                        pe.wait_ge(flag_set, 2)
                        some_lo[0] = pe.value_load(some_inexact[0:1, 0:1], min_val=0, max_val=1)

            iterate(pe, body)

        @block.scalar
        def _(act):
            start(act, head_act, scan_act, tail_act, end_act)
            act.wait_ge(cols_in, 16)
            act.preload_act_table_set(LN_EXP)
            act.activation(A[:, :], c_("A_log", 0, DT * N), ACT.Exp).then_inc(A_made, 1)
            act.wait_ge(A_made, 1)
            act.mul(A[:, :], A[:, :], -1.0).then_inc(A_made, 1)
            act.wait_ge(A_made, 2)

            def round_stage(s):
                w, src, k = STAGES[s]
                n = SC // src.shape[1]
                act.wait_ge(stage_in[s % 3], 16 * (s // 3 + 1))
                act.copy(w[:, k:k + n, :], staging[s % 3].rearrange("p (k n) -> p k n", k=n)).then_inc(stage_hi, 1)

            def front(c, par, n, first):
                if first:
                    act.wait_ge(bcast_pe.sem, bcast_pe.at(c, f"b{n}"))
                    if n >= 1:
                        act.wait_ge(scan_pool.sem, scan_pool.at(c, f"dBu{n - 1}"))
                    else:
                        act.wait_ge(scan_pool.sem, scan_pool.at(c - 1, f"dBu{N - 1}"))
                    act.copy(Bs[:, :], bP[n % 2][:, 0, :]).then_inc(scan_act.sem, 1)
                    if n == 0:
                        act.wait_ge(head_vec.sem, head_vec.at(c, "delta"))
                for d in ((0, 1) if first else (2, 3)):
                    if n >= 2:
                        act.wait_ge(scan_vec.sem, scan_vec.at(c, f"s{d}_{n - 2}"))
                    else:
                        act.wait_ge(scan_vec.sem, scan_vec.at(c - 1, f"s{d}_{N - 2 + n}"))
                    act.activation(dA[n % 2][:, d, :], delta[par][:, d, :], ACT.Exp,
                                   scale=A[:, d * N + n:d * N + n + 1]).then_inc(scan_act.sem, 1)

            def copy_C(c, n):
                if n >= 1:
                    act.wait_ge(scan_vec.sem, scan_vec.at(c, f"g{n - 1}"))
                else:
                    act.wait_ge(scan_vec.sem, scan_vec.at(c - 1, f"g{N - 1}"))
                act.copy(Cs[:, :], bP[n % 2][:, 1, :]).then_inc(scan_act.sem, 1)

            def normed(dst, src, sm, r):
                for t in range(TT):
                    a = act.activation(dst[:, t, :], src[:, t, :], ACT.Identity,
                                       scale=sm[:, r, t:t + 1], bias=sm[:, r + 1, t:t + 1])
                return a

            def head_step(h, hp, hs):
                if hs in (3, 5):
                    i, src, w = (1, 0, "w") if hs == 3 else (2, 6, "w2")
                    act.wait_ge(head_vec.sem, head_vec.at(h, w))
                    act.activation(hsm[:, src + 1, :], hsm[:, src, :], ACT.Ln).then_inc(head_act.sem, 1)
                    act.wait_ge(head_act.sem, head_act.at(h, f"ln{i}"))
                    act.activation(hsm[:, src + 2, :], hsm[:, src + 1, :], ACT.Exp,
                                   scale=-0.5).then_inc(head_act.sem, 1)
                if hs == 7:
                    act.wait_ge(head_vec.sem, head_vec.at(h, "nmr12"))
                    act.wait_ge(head_pool.sem, head_pool.at(h - 1, "log1p"))
                    normed(hn, xh, hsm, 12).then_inc(head_act.sem, 1)
                if hs == 9:
                    act.wait_ge(head_pe.sem, head_pe.at(h, "hT"))
                    for k in range(KM):
                        a = act.activation(hT[:, k, :], hP[0][:, k, :], ACT.Copy, scale=c_("norm_w", k))
                    a.then_inc(head_act.sem, 1)
                if hs in (11, 12):
                    q = hs - 11
                    if q == 0:
                        act.wait_ge(head_vec.sem, head_vec.at(h, "halo"))
                    act.wait_ge(head_pe.sem, head_pe.at(h, f"u{q}"))
                    act.copy(u_ext[:, 2 * q:2 * q + 2, CONV - 1:], hP[(q + 1) % 2][:, :, :]).then_inc(head_act.sem, 1)
                if hs == 13:
                    act.wait_ge(head_act.sem, head_act.at(h, "u1"))
                    act.wait_ge(tail_pe.sem, tail_pe.at(h - 2, "out"))
                    for d in range(DT):
                        a = act.activation(uc[hp][:, d, :], u_ext[:, d, CONV - 1:], ACT.Identity,
                                           scale=c_("conv_w", d * CONV + CONV - 1), bias=c_("conv_b", d))
                    a.then_inc(head_act.sem, 1)
                if hs == 21:
                    act.wait_ge(head_pe.sem, head_pe.at(h, "xp"))
                    act.wait_ge(tail_vec.sem, tail_vec.at(h - 2, "gated1"))
                    act.copy(dtx, hP[1][4 * N:XC, 0, :]).then_inc(head_act.sem, 1)
                if hs in (23, 24):
                    q = hs - 23
                    act.wait_ge(head_pe.sem, head_pe.at(h, "d1"))
                    for i in range(2):
                        d = 2 * q + i
                        act.activation(e_sp[:, d, :], hP[q][:, i, :], ACT.Abs, bias=c_("dt_b", d))
                        a = act.activation(delta[hp][:, d, :], hP[q][:, i, :], ACT.Relu, bias=c_("dt_b", d))
                    a.then_inc(head_act.sem, 1)
                if hs == 24:
                    act.wait_ge(head_act.sem, head_act.at(h, "v1"))
                    act.activation(e_sp[:, :, :], e_sp[:, :, :], ACT.Exp, scale=-1.0).then_inc(head_act.sem, 1)
                if hs == 26:
                    act.wait_ge(head_vec.sem, head_vec.at(h, "res"))
                    act.activation(e_sp[:, :, :], e_sp[:, :, :], ACT.Ln, bias=1.0).then_inc(head_act.sem, 1)

            def silus(h, hp, f, fp, head, tail):
                if head:
                    act.wait_ge(head_vec.sem, head_vec.at(h, "tap2"))
                    act.activation(uc[hp][:, :, :], uc[hp][:, :, :], ACT.Silu).then_inc(head_act.sem, 1)
                    act.wait_ge(head_pe.sem, head_pe.at(h, "z0"))
                    act.activation(z[hp][:, 0:2, :], hP[1][:, :, :], ACT.Silu).then_inc(head_act.sem, 1)
                if tail:
                    act.wait_ge(tail_act.sem, tail_act.at(f, f"a{HM - 1}"))
                    for i in range(2):
                        half = slice(i * HM // 2, (i + 1) * HM // 2)
                        act.activation(Rw[:, half, :], Rw[:, half, :], ACT.Silu).then_inc(tail_act.sem, 1)
                if head:
                    act.wait_ge(head_pe.sem, head_pe.at(h, "z1"))
                    act.activation(z[hp][:, 2:4, :], hP[0][:, :, :], ACT.Silu).then_inc(head_act.sem, 1)
                act.preload_act_table_set(LN_EXP)

            def tail_step(f, fp, hs):
                if hs in (5, 8):
                    s, src = ("o", 0) if hs == 5 else ("x", 5)
                    act.wait_ge(tail_vec.sem, tail_vec.at(f, f"{s}_w"))
                    act.activation(tsm[:, src + 1, :], tsm[:, src, :], ACT.Ln).then_inc(tail_act.sem, 1)
                    act.wait_ge(tail_act.sem, tail_act.at(f, f"{s}_ln"))
                    act.activation(tsm[:, src + 2, :], tsm[:, src + 1, :], ACT.Exp,
                                   scale=-0.5).then_inc(tail_act.sem, 1)
                if hs == 6:
                    act.wait_ge(tail_vec.sem, tail_vec.at(f, "o_nmr"))
                    normed(o, o, tsm, 3).then_inc(tail_act.sem, 1)
                if hs == 10:
                    act.wait_ge(tail_vec.sem, tail_vec.at(f, "x_nmr"))
                    normed(o, x1[fp], tsm, 8).then_inc(tail_act.sem, 1)
                if hs == 12:
                    act.wait_ge(tail_pe.sem, tail_pe.at(f, "xfT"))
                    act.copy(xfT_hi, ring(1 - fp, "xfT")[:, :, :]).then_inc(tail_act.sem, 1)
                if 15 <= hs < 19:
                    if hs == 15:
                        act.wait_ge(end_pool.sem, end_pool.at(f - 1, "lo2_0"))
                        act.wait_ge(end_vec.sem, end_vec.at(f - 1, "lo2_1"))
                    i = hs - 15
                    act.wait_ge(tail_pe.sem, tail_pe.at(f, f"a{i}"))
                    for t in range(2):
                        m = 2 * i + t
                        act.activation(Rw[:, m, :], ring(1 - fp, f"a{i}")[:, t, :], ACT.Copy,
                                       scale=c_("w1_s", m)).then_inc(tail_act.sem, 1)
                if hs == 21:
                    act.wait_ge(tail_vec.sem, tail_vec.at(f, "gated0"))
                    act.wait_ge(end_pe.sem, end_pe.at(f - 1, "w3"))
                    act.copy(Ghi[:, 0:HM // 2, :], Rw[:, 0:HM // 2, :]).then_inc(tail_act.sem, 1)
                if 24 <= hs < 32:
                    m = hs - 24
                    if m == 0:
                        act.wait_ge(tail_pool.sem, tail_pool.at(f, "lo0_0"))
                        act.wait_ge(tail_vec.sem, tail_vec.at(f, "lo0_1"))
                    act.wait_ge(tail_pe.sem, tail_pe.at(f, f"h1_{m}"))
                    act.activation(Rw[:, m, :], ring(1 - fp, f"h1_{m}")[:, 0, :], ACT.Copy,
                                   scale=c_("h1_s", m)).then_inc(tail_act.sem, 1)
                if hs == 31:
                    gelu(f, tail_act, f"h1_{HM - 1}", "gelu1_0", tail_pe)

            def gelu(c, steps, done, first, products):
                act.wait_ge(products.sem, products.at(c, done))
                act.wait_ge(steps.sem, steps.at(c, done))
                low, high = slice(0, HM // 2), slice(HM // 2, HM)
                act.activation(Rw[:, low, :], Rw[:, low, :], ACT.Gelu).then_inc(steps.sem, 1)
                act.wait_ge(steps.sem, steps.at(c, first))
                act.copy(Ghi[:, low, :], Rw[:, low, :]).then_inc(steps.sem, 1)
                act.activation(Rw[:, high, :], Rw[:, high, :], ACT.Gelu).then_inc(steps.sem, 1)
                act.preload_act_table_set(LN_EXP)

            def end_step(g, gp, hs):
                if 4 <= hs < 12:
                    m = hs - 4
                    if m == 0:
                        act.wait_ge(end_pool.sem, end_pool.at(g, "lo1_0"))
                        act.wait_ge(end_vec.sem, end_vec.at(g, "lo1_1"))
                    act.wait_ge(end_pe.sem, end_pe.at(g, f"h2_{m}"))
                    act.activation(Rw[:, m, :], ring(gp, f"h2_{m}")[:, 0, :], ACT.Copy,
                                   scale=c_("h2_s", m)).then_inc(end_act.sem, 1)
                if hs == 11:
                    gelu(g, end_act, f"h2_{HM - 1}", "gelu2_0", end_pe)
                if hs == 16:
                    act.wait_ge(end_vec.sem, end_vec.at(g, "w"))
                    act.activation(fsm[:, 1, :], fsm[:, 0, :], ACT.Ln).then_inc(end_act.sem, 1)
                    act.wait_ge(end_act.sem, end_act.at(g, "ln"))
                    act.activation(fsm[:, 2, :], fsm[:, 1, :], ACT.Exp, scale=-0.5).then_inc(end_act.sem, 1)
                if hs == 18:
                    act.wait_ge(end_vec.sem, end_vec.at(g, "nmr"))
                    normed(o, o, fsm, 3).then_inc(end_act.sem, 1)

            def body(c, par, scan=False, head=False, tail=False, end=False, prepare=False,
                     seq_start=None, head_seq_start=None, j=None):
                for hs in range(HALVES):
                    n = hs // 2
                    if scan and hs % 2 == 0:
                        copy_C(c, n)
                    if scan and n + 1 < N:
                        front(c, par, n + 1, hs % 2 == 0)
                    if head and hs >= HALVES - 2:
                        front(c + 1, 1 - par, 0, hs % 2 == 0)
                    if end:
                        end_step(c - 2, par, hs)
                    if tail:
                        tail_step(c - 1, 1 - par, hs)
                    if head:
                        head_step(c + 1, 1 - par, hs)
                    if hs == 19:
                        silus(c + 1, 1 - par, c - 1, 1 - par, head, tail)
                    for s in stages_at(c, hs):
                        round_stage(s)

            iterate(act, body)

        @block.vector
        def _(dve):
            start(dve, head_vec, scan_vec, tail_vec, end_vec)
            dve.memset(carry[:, :, :], 0.0).then_inc(carry_clear, 1)
            dve.wait_ge(carry_clear, 1)
            dve.wait_ge(ident_made, 3)
            dve.tensor_tensor(pick[:, :], ident[0:4 * N, 0:2 * N], ident[0:4 * N, 2 * N:4 * N],
                              ALU.add).then_inc(pick_made, 1)
            dve.wait_ge(cols_in, 16)

            def mark_stage(s):
                w, src, k = STAGES[s]
                n = SC // src.shape[1]
                dve.wait_ge(stage_hi, s + 1)
                tile = staging[s % 3].rearrange("p (k n) -> p k n", k=n)
                dve.tensor_tensor(tile, tile, w[:, k:k + n, :].bitcast(F32), ALU.not_equal).then_inc(stage_marked, 1)

            def newton(steps, c, names, sm, src, y):
                w, l, g = sm[:, src, :], sm[:, src + 1, :], sm[:, src + 2, :]
                dve.scalar_tensor_tensor(l, g, -0.5, g, ALU.mult, ALU.mult).then_inc(steps.sem, 1)
                dve.wait_ge(steps.sem, steps.at(c, names[0]))
                dve.tensor_tensor(l, l, w, ALU.mult).then_inc(steps.sem, 1)
                dve.wait_ge(steps.sem, steps.at(c, names[1]))
                dve.scalar_tensor_tensor(y, l, 1.5, g, ALU.add, ALU.mult).then_inc(steps.sem, 1)
                dve.wait_ge(steps.sem, steps.at(c, names[2]))

            def stats(steps, c, names, src, stat, mv, w):
                for t in range(TT):
                    a = dve.bn_stats(stat[:, t, :], src[:, t, :])
                a.then_inc(steps.sem, 1)
                dve.wait_ge(steps.sem, steps.at(c, names[0]))
                dve.memset(gate[:, :], 0.0)
                for t in range(TT):
                    a = dve.bn_aggr(mv[:, t, :], stat[:, t, :])
                a.then_inc(steps.sem, 1)
                dve.wait_ge(steps.sem, steps.at(c, names[1]))
                dve.tensor_scalar(w, mv[:, :, 1], LN_EPS, None, ALU.add).then_inc(steps.sem, 1)

            def minus_mean(dst, mv, r):
                return dve.scalar_tensor_tensor(dst, mv[:, :, 0], -1.0, r, ALU.mult, ALU.mult)

            def back(c, par, n, first):
                s = S[slot(par, n)]
                if first:
                    dve.wait_ge(scan_pool.sem, scan_pool.at(c, f"dBu{n}"))
                for d in ((0, 1) if first else (2, 3)):
                    dve.wait_ge(scan_act.sem, scan_act.at(c, f"e{d}_{n}"))
                    dve.tensor_tensor_scan(s[:, d, :], dA[n % 2][:, d, :], s[:, d, :],
                                           carry[:, n, d:d + 1], ALU.mult, ALU.add).then_inc(scan_vec.sem, 1)
                if not first:
                    dve.wait_ge(scan_vec.sem, scan_vec.at(c, f"s{DT - 1}_{n}"))
                    dve.tensor_copy(carry[:, n, :], s[:, :, T - 1]).then_inc(scan_vec.sem, 1)
                    dve.wait_ge(scan_vec.sem, scan_vec.at(c, f"carry{n}"))
                    dve.wait_ge(scan_act.sem, scan_act.at(c, f"c{n}"))
                    dve.tensor_tensor(s[:, :, :], s[:, :, :], Cs[:, None, :].broadcast_to([P, DT, T]),
                                      ALU.mult).then_inc(scan_vec.sem, 1)

            def head_step(h, hp, hs, first):
                if hs == 3:
                    dve.wait_ge(xh_in.sem, xh_in.at(h, "landed"))
                    stats(head_vec, h, ("x_stats", "x_aggr"), xh, hstat, hmv, hsm[:, 0, :])
                if hs == 4:
                    r1 = mr[hp][:, 0, :]
                    dve.wait_ge(head_act.sem, head_act.at(h, "ex1"))
                    newton(head_vec, h, ("n1", "n2", "r1"), hsm, 0, r1)
                    dve.tensor_tensor(hsm[:, 5, :], r1, r1, ALU.mult).then_inc(head_vec.sem, 1)
                    dve.wait_ge(head_vec.sem, head_vec.at(h, "q1"))
                    dve.tensor_tensor(hsm[:, 5, :], hsm[:, 5, :], hmv[:, :, 1], ALU.mult).then_inc(head_vec.sem, 1)
                    dve.wait_ge(head_vec.sem, head_vec.at(h, "q2"))
                    dve.tensor_scalar(hsm[:, 6, :], hsm[:, 5, :], RMS_EPS, None, ALU.add).then_inc(head_vec.sem, 1)
                    minus_mean(mr[hp][:, 1, :], hmv, r1).then_inc(head_vec.sem, 1)
                if hs == 6:
                    dve.wait_ge(head_act.sem, head_act.at(h, "ex2"))
                    newton(head_vec, h, ("m1", "m2", "r2"), hsm, 6, hsm[:, 9, :])
                    dve.tensor_tensor(hsm[:, 12, :], mr[hp][:, 0, :], hsm[:, 9, :], ALU.mult).then_inc(head_vec.sem, 1)
                    dve.wait_ge(head_vec.sem, head_vec.at(h, "r12"))
                    minus_mean(hsm[:, 13, :], hmv, hsm[:, 12, :]).then_inc(head_vec.sem, 1)
                if hs == 10:
                    ahead, last = u_ext[:, :, 0:CONV - 1], u_ext[:, :, T:T + CONV - 1]
                    if isinstance(first, bool):
                        if first:
                            dve.memset(ahead, 0.0).then_inc(head_vec.sem, 1)
                        else:
                            dve.tensor_copy(ahead, last).then_inc(head_vec.sem, 1)
                    else:
                        with dve.If(first):
                            dve.memset(ahead, 0.0).then_inc(head_vec.sem, 1)
                        with dve.Else():
                            dve.tensor_copy(ahead, last).then_inc(head_vec.sem, 1)
                if hs in (14, 15, 16):
                    k = hs - 14
                    if k == 0:
                        dve.wait_ge(head_act.sem, head_act.at(h, "cbase"))
                    else:
                        dve.wait_ge(head_vec.sem, head_vec.at(h, f"tap{k - 1}"))
                    for d in range(DT):
                        a = dve.scalar_tensor_tensor(uc[hp][:, d, :], u_ext[:, d, k:k + T],
                                                     c_("conv_w", d * CONV + k), uc[hp][:, d, :], ALU.mult, ALU.add)
                    a.then_inc(head_vec.sem, 1)
                if hs == 21:
                    dve.wait_ge(head_act.sem, head_act.at(h, "dtx"))
                    dve.tensor_copy(BC[hp][:, :], hP[1][0:4 * N, 0, :]).then_inc(head_vec.sem, 1)
                    dve.wait_ge(head_vec.sem, head_vec.at(h, "bc_hi"))
                    lo = slice(2 * N, 4 * N)
                    dve.tensor_tensor(BC[hp][lo, :], hP[1][lo, 0, :], BC[hp][lo, :].bitcast(F32),
                                      ALU.subtract).then_inc(head_vec.sem, 1)
                if hs == 25:
                    dve.wait_ge(head_act.sem, head_act.at(h, "e"))
                    dve.tensor_scalar(X[hp][:, :, :], e_sp[:, :, :], 1.0, -1.0,
                                      ALU.add, ALU.add).then_inc(head_vec.sem, 1)
                    dve.wait_ge(head_vec.sem, head_vec.at(h, "t1"))
                    dve.tensor_tensor(X[hp][:, :, :], e_sp[:, :, :], X[hp][:, :, :],
                                      ALU.subtract).then_inc(head_vec.sem, 1)
                if hs == 28:
                    dve.wait_ge(head_pool.sem, head_pool.at(h, "log1p"))
                    dve.tensor_tensor(delta[hp][:, :, :], delta[hp][:, :, :], X[hp][:, :, :],
                                      ALU.add).then_inc(head_vec.sem, 1)

            low, high = slice(0, HM // 2), slice(HM // 2, HM)

            def split_high(before, c, name, steps, hi):
                dve.wait_ge(before.sem, before.at(c, name))
                dve.tensor_copy(Ghi[:, high, :], Rw[:, high, :]).then_inc(steps.sem, 1)
                dve.wait_ge(steps.sem, steps.at(c, hi))
                dve.tensor_tensor(Glo[:, high, :], Rw[:, high, :], Ghi[:, high, :].bitcast(F32),
                                  ALU.subtract).then_inc(steps.sem, 1)

            def split_input(f, fp):
                dve.wait_ge(tail_act.sem, tail_act.at(f, "xf_hi"))
                dve.wait_ge(end_pe.sem, end_pe.at(f - 1, "w3"))
                dve.tensor_tensor(xfT_lo, ring(1 - fp, "xfT")[:, :, :], xfT_hi.bitcast(F32),
                                  ALU.subtract).then_inc(tail_vec.sem, 1)

            def tail_step(f, fp, hs, head):
                if hs == 0:
                    dve.wait_ge(sum_pe.sem, sum_pe.at(f, f"y{N - 1}"))
                    for d in range(DT):
                        a = dve.scalar_tensor_tensor(uc[fp][:, d, :], uc[fp][:, d, :], c_("D", d), yP[:, d, :],
                                                     ALU.mult, ALU.add)
                    a.then_inc(tail_vec.sem, 1)
                    dve.wait_ge(tail_vec.sem, tail_vec.at(f, "y_d"))
                    dve.tensor_tensor(z[fp][:, :, :], uc[fp][:, :, :], z[fp][:, :, :],
                                      ALU.mult).then_inc(tail_vec.sem, 1)
                if hs == 4:
                    dve.wait_ge(xt_in.sem, xt_in.at(f, "landed"))
                    dve.wait_ge(tail_pe.sem, tail_pe.at(f, "out"))
                    for t in range(TT):
                        a = dve.scalar_tensor_tensor(o[:, t, :], xt[:, t, :], mr[fp][:, 0, t:t + 1],
                                                     ring(1 - fp, "out")[:, t, :], ALU.mult, ALU.add)
                    a.then_inc(tail_vec.sem, 1)
                    dve.wait_ge(tail_vec.sem, tail_vec.at(f, "o_mul"))
                    for t in range(TT):
                        a = dve.tensor_scalar(o[:, t, :], o[:, t, :], mr[fp][:, 1, t:t + 1], None, ALU.add)
                    a.then_inc(tail_vec.sem, 1)
                    dve.wait_ge(tail_vec.sem, tail_vec.at(f, "o_add"))
                    stats(tail_vec, f, ("o_stats", "o_aggr"), o, tstat, tmv, tsm[:, 0, :])
                if hs == 5:
                    dve.wait_ge(tail_act.sem, tail_act.at(f, "o_ex"))
                    newton(tail_vec, f, ("o_n1", "o_n2", "o_r"), tsm, 0, tsm[:, 3, :])
                    minus_mean(tsm[:, 4, :], tmv, tsm[:, 3, :]).then_inc(tail_vec.sem, 1)
                if hs == 7:
                    dve.wait_ge(tail_act.sem, tail_act.at(f, "o_norm"))
                    dve.wait_ge(out_stored.sem, out_stored.at(f - 2, "landed"))
                    dve.tensor_tensor(x1[fp][:, :, :], xt[:, :, :], o[:, :, :], ALU.add).then_inc(tail_vec.sem, 1)
                    dve.wait_ge(tail_vec.sem, tail_vec.at(f, "x1"))
                    stats(tail_vec, f, ("x_stats", "x_aggr"), x1[fp], tstat, tmv, tsm[:, 5, :])
                if hs == 9:
                    dve.wait_ge(tail_act.sem, tail_act.at(f, "x_ex"))
                    newton(tail_vec, f, ("x_n1", "x_n2", "x_r"), tsm, 5, tsm[:, 8, :])
                    minus_mean(tsm[:, 9, :], tmv, tsm[:, 8, :]).then_inc(tail_vec.sem, 1)
                if 16 <= hs < 20:
                    i = hs - 16
                    if 2 * i == HM // 2 and head:
                        dve.wait_ge(head_pe.sem, head_pe.at(f + 2, "z1"))
                    dve.wait_ge(tail_pe.sem, tail_pe.at(f, f"b{i}"))
                    for t in range(2):
                        m = 2 * i + t
                        dve.tensor_scalar((X[fp], e_sp)[m // DT][:, m % DT, :], ring(1 - fp, f"b{i}")[:, t, :],
                                          c_("w2_s", m), None, ALU.mult).then_inc(tail_vec.sem, 1)
                if hs == 20:
                    dve.wait_ge(tail_act.sem, tail_act.at(f, "silu0"))
                    dve.wait_ge(tail_vec.sem, tail_vec.at(f, f"b{HM - 1}"))
                    dve.tensor_tensor(Rw[:, low, :], Rw[:, low, :], X[fp][:, :, :], ALU.mult).then_inc(tail_vec.sem, 1)
                    dve.wait_ge(tail_act.sem, tail_act.at(f, "silu1"))
                    dve.tensor_tensor(Rw[:, high, :], Rw[:, high, :], e_sp[:, :, :], ALU.mult).then_inc(tail_vec.sem, 1)
                    dve.wait_ge(end_pe.sem, end_pe.at(f - 1, "w3"))
                    split_high(tail_vec, f, "gated1", tail_vec, "hi0_1")

            def end_step(g, gp, hs):
                if hs == 1:
                    split_high(tail_act, g, "gelu1_1", end_vec, "hi1_1")
                if hs == 13:
                    split_high(end_act, g, "gelu2_1", end_vec, "hi2_1")
                if hs == 15:
                    dve.wait_ge(end_pe.sem, end_pe.at(g, "w3"))
                    dve.tensor_tensor(o[:, :, :], ring(gp, "w3")[:, :, :],
                                      s_3[:, None, :].broadcast_to([P, TT, DM]), ALU.mult).then_inc(end_vec.sem, 1)
                    dve.wait_ge(end_vec.sem, end_vec.at(g, "out"))
                    stats(end_vec, g, ("stats", "aggr"), o, fstat, fmv, fsm[:, 0, :])
                if hs == 17:
                    dve.wait_ge(end_act.sem, end_act.at(g, "ex"))
                    newton(end_vec, g, ("n1", "n2", "r"), fsm, 0, fsm[:, 3, :])
                    minus_mean(fsm[:, 4, :], fmv, fsm[:, 3, :]).then_inc(end_vec.sem, 1)
                if hs == 19:
                    dve.wait_ge(end_act.sem, end_act.at(g, "norm"))
                    dve.tensor_tensor(x1[gp][:, :, :], x1[gp][:, :, :], o[:, :, :], ALU.add).then_inc(end_vec.sem, 1)

            def body(c, par, scan=False, head=False, tail=False, end=False, prepare=False,
                     seq_start=None, head_seq_start=None, j=None):
                if seq_start is not None:
                    with dve.If(seq_start):
                        dve.memset(carry[:, :, :], 0.0).then_inc(carry_clear, 1)
                    with dve.Else():
                        dve.memset(gate[:, :], 0.0).then_inc(carry_clear, 1)
                    dve.wait_ge(carry_clear, j + 2)
                for hs in range(HALVES):
                    if scan:
                        back(c, par, hs // 2, hs % 2 == 0)
                    if tail and hs == 15:
                        split_input(c - 1, 1 - par)
                    if end:
                        end_step(c - 2, par, hs)
                    if tail:
                        tail_step(c - 1, 1 - par, hs, head)
                    if head:
                        head_step(c + 1, 1 - par, hs, prepare if head_seq_start is None else head_seq_start)
                    if prepare and hs == HALVES - 1:
                        dve.wait_ge(late_in, 16 * LATE)
                    for s in stages_at(c, hs):
                        mark_stage(s)
                    if isinstance(c, int) and c == 0 and hs == HALVES - 1:
                        dve.wait_ge(stage_counted, len(STAGES))
                        dve.tensor_reduce(inexact[:, 0:1], counts, AX.X, ALU.add).then_inc(flag_set, 1)
                        dve.wait_ge(flag_set, 1)
                        dve.tensor_scalar(some_inexact[:, :], inexact[:, 0:1], 0.0, None,
                                          ALU.is_gt).then_inc(flag_set, 1)

            iterate(dve, body)


def kernel(**inputs):
    import numpy as _np
    import concourse.bacc as _bacc
    from concourse import mybir as _mybir
    from concourse.bass_utils import run_bass_kernel_spmd as _run

    p = 128
    a = {k: _np.asarray(v) for k, v in inputs.items()}
    A, F = "L0_attn_", "L0_ffn_"

    def tiles(v):
        return v.reshape(v.shape[0] // p, p, -1).transpose(1, 0, 2).reshape(p, -1)

    arrays = {
        "x": a[A + "x"],
        "in_proj": a[A + "in_proj_w"].T, "x_proj": a[A + "x_proj_w"].T,
        "dt_proj": a[A + "dt_proj_w"].T, "out_proj": a[A + "out_proj_w"].T,
        "w1": a[F + "w1_w"].T, "w2": a[F + "w2_w"].T,
        "h1": a[F + "h1_w"].T, "h2": a[F + "h2_w"].T, "w3": a[F + "w3_w"].T,
        "cols": _np.concatenate([tiles(a[k]) for k in (
            A + "conv_w", A + "conv_b", A + "dt_proj_b", A + "D", A + "A_log", A + "norm_w",
            F + "w1_s", F + "w2_s", F + "h1_s", F + "h2_s")], axis=1),
        "w3_s": a[F + "w3_s"],
    }
    arrays = {f"in_{k}": _np.ascontiguousarray(v) for k, v in arrays.items()}
    nc = _bacc.Bacc("TRN2", target_bir_lowering=False, num_devices=1)
    args = [nc.dram_tensor(k, v.shape, _mybir.dt.from_np(v.dtype), kind="ExternalInput").ap()
            for k, v in arrays.items()]
    args.append(nc.dram_tensor("out_0", a[A + "x"].shape, _mybir.dt.float32, kind="ExternalOutput").ap())
    build(nc, *args)
    r = _run(nc, [arrays], core_ids=[0])
    return r.results[0]["out_0"]
```
